# Optimizing a Trainium2 kernel written in Bass

```python
import numpy as np
import jax
import jax.numpy as jnp

def _softmax(x, axis=-1):
    return jax.nn.softmax(x, axis=axis)

def _gelu(x):
    return jax.nn.gelu(x, approximate=True)

def _silu(x):
    return jax.nn.silu(x)

def _sigmoid(x):
    return jax.nn.sigmoid(x)

def _layernorm(x, axis=-1, eps=1e-05):
    m = jnp.mean(x, axis=axis, keepdims=True)
    v = jnp.var(x, axis=axis, keepdims=True)
    return (x - m) / jnp.sqrt(v + eps)

def _scatter_add(tgt, idx, src, axis=0):
    return tgt.at[idx].add(src)

def _segment_sum(src, seg, n):
    return jax.ops.segment_sum(src, seg, n)
kernel_name = 'mk_cond_resid_d4_seqx_r4_9c0c0f'

def setup_inputs(seed: int=0):
    np.random.seed(seed)
    _w = jnp.asarray

    def _rec_inputs():
        import jax
        import jax.numpy as jnp
        _rk = jax.random.key(seed)
        x = -7.109e-05 + 0.9999 * jax.random.normal(jax.random.fold_in(_rk, 1), (32, 64, 512), jnp.float32)
        _lenS = 64 - jax.random.randint(jax.random.fold_in(_rk, 7), (32,), 0, max(1, 64 // 4) + 1, jnp.int32)
        _lenS2 = 64 - jax.random.randint(jax.random.fold_in(_rk, 8), (32,), 0, max(1, 64 // 4) + 1, jnp.int32)
        itok_B_1_198 = jax.random.randint(jax.random.fold_in(_rk, 11), (32,), 1, 199, jnp.int32)
        itok_B_0_3 = jax.random.randint(jax.random.fold_in(_rk, 12), (32,), 0, 4, jnp.int32)
        itok_B_0_6 = jax.random.randint(jax.random.fold_in(_rk, 13), (32,), 0, 7, jnp.int32)
        itok_Bx257_0_4111 = jax.random.randint(jax.random.fold_in(_rk, 14), (32, 257), 0, 1028, jnp.int32)
        itok_B_37_3939 = jax.random.randint(jax.random.fold_in(_rk, 15), (32,), 37, 985, jnp.int32)
        return (x, itok_B_1_198, itok_B_0_3, itok_B_0_6, itok_Bx257_0_4111, itok_B_37_3939)
    x, itok_B_1_198, itok_B_0_3, itok_B_0_6, itok_Bx257_0_4111, itok_B_37_3939 = _rec_inputs()

    def _L0_cond_setup():
        import jax, jax.numpy as jnp
        import numpy as np
        B, C, T = (128, 64, 512)
        S, D = (200, 64)
        key = jax.random.key(seed)
        k1, k2, k3 = jax.random.split(key, 3)
        x = jax.random.normal(k1, (B, C, T), dtype=jnp.float32)
        conditions = jax.random.randint(k2, (B,), 0, S, dtype=jnp.int64)
        weights = jax.random.normal(k3, (S, C, D), dtype=jnp.float32) / jnp.sqrt(jnp.float32(C))
        return {'x': x, 'conditions': conditions, 'weights': weights}
    _L0_cond_all = _L0_cond_setup()
    _L0_cond_in = {k: v for k, v in _L0_cond_all.items() if k in ('weights',)}
    del _L0_cond_all

    def _L1_cond_setup():
        import jax, jax.numpy as jnp
        import numpy as np
        B, S, D_IN, D_OUT, R, E = (8, 512, 512, 512, 16, 4)
        key = jax.random.key(seed)
        ks = jax.random.split(key, 7)
        x = jax.random.normal(ks[0], (B, S, D_IN), dtype=jnp.float32)
        W_base = jax.random.normal(ks[1], (D_OUT, D_IN), dtype=jnp.float32) * 0.02
        Wt = jax.random.normal(ks[2], (D_IN, D_IN), dtype=jnp.float32) * 0.02
        A = jax.random.normal(ks[3], (E, R, D_IN), dtype=jnp.float32) * 0.02
        B_w = jax.random.normal(ks[4], (E, D_OUT, R), dtype=jnp.float32) * 0.02
        Wp = jax.random.normal(ks[5], (D_OUT, D_OUT), dtype=jnp.float32) * 0.02
        scaling = jnp.ones((E,), dtype=jnp.float32)
        adapter_idx = jax.random.randint(ks[6], (B,), 0, E)
        return {'x': x, 'W_base': W_base, 'Wt': Wt, 'A': A, 'B_w': B_w, 'Wp': Wp, 'scaling': scaling, 'adapter_idx': adapter_idx}
    _L1_cond_all = _L1_cond_setup()
    _L1_cond_in = {k: v for k, v in _L1_cond_all.items() if k in ('W_base', 'Wt', 'A', 'B_w', 'Wp', 'scaling')}
    del _L1_cond_all

    def _L2_cond_setup():
        import jax, jax.numpy as jnp
        import numpy as np
        B, T, D_IN, D_OUT = (16, 512, 512, 512)
        N_ADAPTERS, RANK = (8, 16)
        key = jax.random.key(seed)
        k_x, k_w, k_a, k_b, k_s, k_idx = jax.random.split(key, 6)
        x = jax.random.normal(k_x, (B, T, D_IN), dtype=jnp.float32)
        W = jax.random.normal(k_w, (D_OUT, D_IN), dtype=jnp.float32) * (1.0 / np.sqrt(D_IN))
        A = jax.random.normal(k_a, (N_ADAPTERS, RANK, D_IN), dtype=jnp.float32) * 0.02
        Bm = jax.random.normal(k_b, (N_ADAPTERS, D_OUT, RANK), dtype=jnp.float32) * 0.02
        scalings = jnp.ones((N_ADAPTERS,), dtype=jnp.float32)
        adapter_idx = jax.random.randint(k_idx, (B,), 0, N_ADAPTERS, dtype=jnp.int32)
        return {'x': x, 'W': W, 'A': A, 'Bm': Bm, 'scalings': scalings, 'adapter_idx': adapter_idx}
    _L2_cond_all = _L2_cond_setup()
    _L2_cond_in = {k: v for k, v in _L2_cond_all.items() if k in ('W', 'A', 'Bm', 'scalings')}
    del _L2_cond_all

    def _L3_cond_setup():
        import jax, jax.numpy as jnp
        import numpy as np
        H, G, HD = (8, 4, 64)
        GSZ = H // G
        BLOCK = 16
        WINDOW = 256
        SCALE = 256.0 ** (-0.5)
        EPS = 1e-06
        THETA = 10000.0
        B, T, D = (16, 4, 512)
        NBLK = 257

        def _rms(x, scale):
            var = jnp.mean(x * x, axis=-1, keepdims=True)
            return x * jax.lax.rsqrt(var + EPS) * (1.0 + scale)

        def _rope(x, pos):
            half = HD // 2
            inv = 1.0 / THETA ** (jnp.arange(half, dtype=jnp.float32) / half)
            ang = pos[:, :, None].astype(jnp.float32) * inv
            cos = jnp.cos(ang)[:, None, :, :]
            sin = jnp.sin(ang)[:, None, :, :]
            x1, x2 = (x[..., :half], x[..., half:])
            return jnp.concatenate([x1 * cos - x2 * sin, x2 * cos + x1 * sin], axis=-1)
        key = jax.random.key(seed)
        ks = jax.random.split(key, 10)
        inv_d = 1.0 / np.sqrt(D)
        return {'x': jax.random.normal(ks[0], (B, T, D), jnp.float32), 'Wq': jax.random.normal(ks[1], (H * HD, D), jnp.float32) * inv_d, 'Wk': jax.random.normal(ks[2], (G * HD, D), jnp.float32) * inv_d, 'Wv': jax.random.normal(ks[3], (G * HD, D), jnp.float32) * inv_d, 'Wo': jax.random.normal(ks[4], (D, H * HD), jnp.float32) * inv_d, 'q_norm_scale': jax.random.normal(ks[5], (HD,), jnp.float32) * 0.02, 'k_norm_scale': jax.random.normal(ks[6], (HD,), jnp.float32) * 0.02, 'k_blocks': jax.random.normal(ks[7], (B * NBLK, G, BLOCK, HD), jnp.float32), 'v_blocks': jax.random.normal(ks[8], (B * NBLK, G, BLOCK, HD), jnp.float32), 'block_tables': jnp.arange(B * NBLK, dtype=jnp.int32).reshape(B, NBLK), 'kv_lens': jax.random.randint(ks[9], (B,), 0, 1024, dtype=jnp.int32)}
    _L3_cond_all = _L3_cond_setup()
    _L3_cond_in = {k: v for k, v in _L3_cond_all.items() if k in ('Wq', 'Wk', 'Wv', 'Wo', 'q_norm_scale', 'k_norm_scale', 'k_blocks', 'v_blocks')}
    del _L3_cond_all
    return {'x': x, 'itok_B_1_198': itok_B_1_198, 'itok_B_0_3': itok_B_0_3, 'itok_B_0_6': itok_B_0_6, 'itok_Bx257_0_4111': itok_Bx257_0_4111, 'itok_B_37_3939': itok_B_37_3939, 'L0_cond_weights': _L0_cond_in['weights'], 'L1_cond_W_base': _L1_cond_in['W_base'], 'L1_cond_Wt': _L1_cond_in['Wt'], 'L1_cond_A': _L1_cond_in['A'], 'L1_cond_B_w': _L1_cond_in['B_w'], 'L1_cond_Wp': _L1_cond_in['Wp'], 'L1_cond_scaling': _L1_cond_in['scaling'], 'L2_cond_W': _L2_cond_in['W'], 'L2_cond_A': _L2_cond_in['A'], 'L2_cond_Bm': _L2_cond_in['Bm'], 'L2_cond_scalings': _L2_cond_in['scalings'], 'L3_cond_Wq': _L3_cond_in['Wq'], 'L3_cond_Wk': _L3_cond_in['Wk'], 'L3_cond_Wv': _L3_cond_in['Wv'], 'L3_cond_Wo': _L3_cond_in['Wo'], 'L3_cond_q_norm_scale': _L3_cond_in['q_norm_scale'], 'L3_cond_k_norm_scale': _L3_cond_in['k_norm_scale'], 'L3_cond_k_blocks': _L3_cond_in['k_blocks'], 'L3_cond_v_blocks': _L3_cond_in['v_blocks']}

def reference(x, itok_B_1_198, itok_B_0_3, itok_B_0_6, itok_Bx257_0_4111, itok_B_37_3939, L0_cond_weights, L1_cond_W_base, L1_cond_Wt, L1_cond_A, L1_cond_B_w, L1_cond_Wp, L1_cond_scaling, L2_cond_W, L2_cond_A, L2_cond_Bm, L2_cond_scalings, L3_cond_Wq, L3_cond_Wk, L3_cond_Wv, L3_cond_Wo, L3_cond_q_norm_scale, L3_cond_k_norm_scale, L3_cond_k_blocks, L3_cond_v_blocks):
    import jax
    import jax.numpy as jnp

    def _L0_cond_ref(x, conditions, weights):
        import jax, jax.numpy as jnp
        import numpy as np
        B, C, T = (128, 64, 512)
        S, D = (200, 64)
        w = weights[conditions]
        return jnp.einsum('bct,bcd->bdt', x, w)

    def _L1_cond_ref(x, W_base, Wt, A, B_w, Wp, scaling, adapter_idx):
        import jax, jax.numpy as jnp
        import numpy as np
        B, S, D_IN, D_OUT, R, E = (8, 512, 512, 512, 16, 4)
        base = jnp.einsum('bsi,oi->bso', x, W_base)
        h = jnp.einsum('bsi,ji->bsj', x, Wt)
        Ab = A[adapter_idx]
        Bb = B_w[adapter_idx]
        sc = scaling[adapter_idx]
        z = jnp.einsum('bsj,brj->bsr', h, Ab)
        l = jnp.einsum('bsr,bor->bso', z, Bb)
        lora_out = jnp.einsum('bso,po->bsp', l, Wp) * sc[:, None, None]
        return base + lora_out

    def _L2_cond_ref(x, W, A, Bm, scalings, adapter_idx):
        import jax, jax.numpy as jnp
        import numpy as np
        B, T, D_IN, D_OUT = (16, 512, 512, 512)
        N_ADAPTERS, RANK = (8, 16)
        H = jnp.einsum('btd,od->bto', x, W)
        A_b = A[adapter_idx]
        B_b = Bm[adapter_idx]
        s_b = scalings[adapter_idx]
        xa = jnp.einsum('btd,brd->btr', x, A_b)
        delta = jnp.einsum('btr,bor->bto', xa, B_b)
        delta = jax.lax.stop_gradient(delta * s_b[:, None, None])
        return H + delta

    def _L3_cond_ref(x, Wq, Wk, Wv, Wo, q_norm_scale, k_norm_scale, k_blocks, v_blocks, block_tables, kv_lens):
        import jax, jax.numpy as jnp
        import numpy as np
        H, G, HD = (8, 4, 64)
        GSZ = H // G
        BLOCK = 16
        WINDOW = 256
        SCALE = 256.0 ** (-0.5)
        EPS = 1e-06
        THETA = 10000.0
        B, T, D = (16, 4, 512)
        NBLK = 257

        def _rms(x, scale):
            var = jnp.mean(x * x, axis=-1, keepdims=True)
            return x * jax.lax.rsqrt(var + EPS) * (1.0 + scale)

        def _rope(x, pos):
            half = HD // 2
            inv = 1.0 / THETA ** (jnp.arange(half, dtype=jnp.float32) / half)
            ang = pos[:, :, None].astype(jnp.float32) * inv
            cos = jnp.cos(ang)[:, None, :, :]
            sin = jnp.sin(ang)[:, None, :, :]
            x1, x2 = (x[..., :half], x[..., half:])
            return jnp.concatenate([x1 * cos - x2 * sin, x2 * cos + x1 * sin], axis=-1)
        Bx, Tx, _ = x.shape
        q = jnp.einsum('btd,od->bto', x, Wq).reshape(Bx, Tx, H, HD).transpose(0, 2, 1, 3)
        k = jnp.einsum('btd,od->bto', x, Wk).reshape(Bx, Tx, G, HD).transpose(0, 2, 1, 3)
        v = jnp.einsum('btd,od->bto', x, Wv).reshape(Bx, Tx, G, HD).transpose(0, 2, 1, 3)
        q = _rms(q, q_norm_scale)
        k = _rms(k, k_norm_scale)
        pos = kv_lens[:, None] + jnp.arange(Tx, dtype=jnp.int32)
        q = _rope(q, pos)
        k = _rope(k, pos)
        slot = pos // BLOCK
        off = pos % BLOCK
        blk = jnp.take_along_axis(block_tables, slot, axis=1)
        k_blocks = k_blocks.at[blk, :, off, :].set(k.transpose(0, 2, 1, 3))
        v_blocks = v_blocks.at[blk, :, off, :].set(v.transpose(0, 2, 1, 3))
        k_all = k_blocks[block_tables].transpose(0, 2, 1, 3, 4).reshape(Bx, G, -1, HD)
        v_all = v_blocks[block_tables].transpose(0, 2, 1, 3, 4).reshape(Bx, G, -1, HD)
        S = k_all.shape[2]
        qg = q.reshape(Bx, G, GSZ, Tx, HD)
        scores = jnp.einsum('bghtd,bgsd->bghts', qg, k_all) * SCALE
        kpos = jnp.arange(S, dtype=jnp.int32)
        allowed = (kpos[None, None, :] <= pos[:, :, None]) & (kpos[None, None, :] > pos[:, :, None] - WINDOW)
        scores = jnp.where(allowed[:, None, None, :, :], scores, -jnp.inf)
        p = jax.nn.softmax(scores, axis=-1)
        o = jnp.einsum('bghts,bgsd->bghtd', p, v_all).reshape(Bx, H, Tx, HD)
        o = o.transpose(0, 2, 1, 3).reshape(Bx, Tx, H * HD)
        return jnp.einsum('bto,do->btd', o, Wo)
    x = x + _L0_cond_ref(x, itok_B_1_198, L0_cond_weights)
    x = x + _L1_cond_ref(x, L1_cond_W_base, L1_cond_Wt, L1_cond_A, L1_cond_B_w, L1_cond_Wp, L1_cond_scaling, itok_B_0_3)
    x = x + _L2_cond_ref(x, L2_cond_W, L2_cond_A, L2_cond_Bm, L2_cond_scalings, itok_B_0_6)
    x = x + _L3_cond_ref(x, L3_cond_Wq, L3_cond_Wk, L3_cond_Wv, L3_cond_Wo, L3_cond_q_norm_scale, L3_cond_k_norm_scale, L3_cond_k_blocks, L3_cond_v_blocks, itok_Bx257_0_4111, itok_B_37_3939)
    return x

_drawn_inputs = setup_inputs


def setup_inputs(seed=0):
    import zlib

    import numpy as np

    out = dict(_drawn_inputs(seed))
    spreads = {'L1_cond_scaling': (1.0, 0.6), 'L2_cond_scalings': (1.0, 0.6)}
    factors = {'L1_cond_Wt': 8.0,
     'L1_cond_A': 8.0,
     'L1_cond_B_w': 8.0,
     'L1_cond_Wp': 8.0,
     'L3_cond_q_norm_scale': 64.0,
     'L3_cond_k_norm_scale': 64.0,
     'L3_cond_k_blocks': 38.096,
     'L1_cond_W_base': 4.362,
     'L3_cond_Wq': 8.0,
     'L3_cond_Wk': 8.0,
     'L3_cond_Wv': 8.0,
     'L3_cond_Wo': 7.269,
     'L3_cond_v_blocks': 8.0}
    for name, (base, spread) in spreads.items():
        noise = np.random.default_rng([zlib.crc32(name.encode()), seed]).standard_normal(out[name].shape)
        drawn = base * np.exp(spread * noise) if base else spread * noise
        out[name] = jnp.asarray(drawn.astype(out[name].dtype))
    for name, factor in factors.items():
        out[name] = (out[name] * factor).astype(out[name].dtype)
    return out
```

```python
from contextlib import ExitStack

import numpy as np

import concourse.bass as bass
from concourse import mybir

F32 = mybir.dt.float32
I32 = mybir.dt.int32
U32 = mybir.dt.uint32
ALU = mybir.AluOpType
ACT = mybir.ActivationFunctionType
AX = mybir.AxisListType

NB, T, D, HD = 32, 64, 512, 64
NPAIR = 16
NG = 4
NBLK = 257
KVROWS = 4112 * 16
RO = 4
SKIP = 65536.0
BIGC = float(2.0 ** 100)
MAGIC = 12582912.0
TWO_PI = 2.0 * np.pi
C1 = 6.28125
C2 = float(np.float32(np.round((TWO_PI - C1) * 2.0 ** 20) / 2.0 ** 20))
C3 = float(np.float32(TWO_PI - C1 - C2))

CF = {}
CI = {}


def _columns(table, widths):
    at = 0
    for name, w in widths:
        table[name] = (at, at + w)
        at += w
    return at


NCF = _columns(CF, [("ident", 128), ("band", 320), ("iotac", 256), ("la", 160), ("lb", 160), ("iota16", 16),
                    ("inv", 32), ("t", 1), ("e", 1), ("m16", 1), ("val", 1), ("m16b", 1), ("valb", 1)])
NCI = _columns(CI, [("cond", 16), ("kvtok", 16), ("idx1", 32), ("idx2", 32), ("kvall", 32), ("kvw", 1),
                    ("c", 1), ("b257", 1)])
FS = {}
NFS = _columns(FS, [("qs", 64), ("ks", 64), ("s1", 1), ("s2", 1)])


class Book:

    def __init__(self, known):
        self.known, self.new, self.count, self.seen, self.sem = known, {}, {}, {}, {}

    def start(self, nc, ctx):
        self.nc, self.ctx = nc, ctx

    def _sem(self, s):
        if s not in self.sem:
            self.sem[s] = self.ctx.enter_context(self.nc.semaphore("s_" + s))
        return self.sem[s]

    def done(self, ins, s, *key):
        n = 1 if s in ("pe", "act", "dve", "pool") else 16
        self.count[s] = self.count.get(s, 0) + n
        ins.then_inc(self._sem(s), n)
        assert key not in self.new, key
        self.new[key] = (s, self.count[s])

    def need(self, eng, who, *key):
        s, v = self.known.get(key, ("pe", 0)) if self.known is not None else ("pe", 0)
        if self.known and key not in self.known:
            raise KeyError(key)
        if self.seen.get((who, s), 0) < v:
            self.seen[(who, s)] = v
            eng.wait_ge(self._sem(s), v)


class Ring:

    def __init__(self, banks):
        self.banks, self.n, self.readers, self.where = banks, 0, [()] * len(banks), {}

    def take(self, need, key, readers):
        i = self.n % len(self.banks)
        self.n += 1
        for r in self.readers[i]:
            need(*r)
        self.readers[i] = readers
        self.where[key] = self.banks[i]
        return self.banks[i]


def program(nc, book, X, W0, WB, WT, AT, BT, WP, W2, A2, V2D, WQKV, WO, KV, TBL, CFD, CID, FSD, SCR, out):
    ctx = ExitStack()
    with ctx:
        book.start(nc, ctx)

        def sb(name, shape, dt=F32):
            return ctx.enter_context(nc.sbuf_tensor(name, shape, dt))

        psum = [ctx.enter_context(nc.psum_tensor(f"ps{i}", [128, 512], F32)) for i in range(8)]

        cf = sb("cf", [128, NCF])
        ci = sb("ci", [128, NCI], I32)
        fs = sb("fs", [128, NFS])

        def c(name, p0=0, p1=128):
            a, b = CF[name]
            return cf[p0:p1, a:b]

        def cint(name, p0=0, p1=128):
            a, b = CI[name]
            return ci[p0:p1, a:b]

        def f(name, p0=0, p1=128):
            a, b = FS[name]
            return fs[p0:p1, a:b]

        ident = c("ident")

        x3T = sb("x3T", [128, 4, 2048])
        qT = sb("qT", [128, 16, 512])
        RA = sb("RA", [128, 5 * 2048])
        wq = sb("wq", [128, 4, 1024])
        wo = wq[:, :, 0:512]
        d1 = RA[:, 0:2048].rearrange("p (k n) -> p k n", k=4)
        d2 = RA[:, 2048:4096].rearrange("p (k n) -> p k n", k=4)
        xs = RA[:, 4096:6144].rearrange("p (k n) -> p k n", k=4)
        x1T = RA[:, 6144:8192].rearrange("p (k n) -> p k n", k=4)
        x2T = RA[:, 8192:10240].rearrange("p (k n) -> p k n", k=4)
        wt = x3T[:, :, 1024:1536]
        wp = x3T[:, :, 1536:2048]
        at = sb("at", [128, 4, 64])
        bt = sb("bt", [128, 4, 64])
        v1 = sb("v1", [64, 512])
        v2 = sb("v2", [128, 512])
        z1 = sb("z1", [64, 512])
        z2 = sb("z2", [128, 512])
        stage = qT[:, 8:10, :].rearrange("p a (b n) -> p (a b) n", n=64)
        mk1 = sb("mk1", [64, 32])
        mk2 = sb("mk2", [128, 32])
        w0i = sb("w0i", [128, 16], I32)
        qr = sb("qr", [128, 3, 512])
        tab = {(n, h): sb(f"tab{n}{h}", [128, 16, 2, 32]) for n in "qk" for h in "ab"}
        sq = sb("sq", [128, 512])
        yy = sb("yy", [128, 512])
        t1 = sb("t1", [128, 512])
        t2 = sb("t2", [128, 512])
        ss = sb("ss", [128, 2, 8])
        gg = sb("gg", [128, 4, 2, 32])
        nt = sb("nt", [128, 2, 512])
        KVo = sb("KVo", [128, RO, 4, 512])
        KVn = RA[:, 7744:8768].rearrange("p (r n) -> p r n", r=2)
        lastKV = KVo[:, RO - 1, :, :].rearrange("p a n -> p (a n)")
        w0 = lastKV[:, 0:1024].rearrange("p (a b n) -> p a b n", a=2, b=4)
        u1 = lastKV[:, 1024:1280].rearrange("p (k n) -> p k n", k=4)
        u2 = lastKV[:, 1280:1792].rearrange("p (k n) -> p k n", k=4)
        thr = sb("thr", [128, 32])
        nmx = sb("nmx", [128, 128])
        sm = sb("sm", [128, 128])
        rs = sb("rs", [128, 128])
        io = sb("io", [128, 2, 32], U32)
        iw = sb("iw", [128, 2, 32], U32)
        inw = sb("inw", [128, 16], U32)

        ks = RA[:, 0:1280].rearrange("p (r g n) -> p r g n", r=2, g=2)
        Sp = RA[:, 1280:2240].rearrange("p (r n) -> p r n", r=3)
        Pp = RA[:, 2240:3392].rearrange("p (r n) -> p r n", r=3)
        PT = RA[:, 3392:4544].rearrange("p (r n) -> p r n", r=3)
        Os = RA[:, 4544:5056].rearrange("p (r n) -> p r n", r=2)
        oT = RA[:, 5056:6080].rearrange("p (r g h n) -> p r g h n", r=2, g=2, h=2)
        Fo = RA[:, 6080:7104].rearrange("p (r n) -> p r n", r=2)
        mask = RA[:, 7104:7744].rearrange("p (r n) -> p r n", r=2)

        tmp = qT[:, 10:16, :].rearrange("p a n -> p (a n)")
        E = tmp[0:32, 0:672].rearrange("p (i b) -> p i b", b=32)
        MA = tmp[:, 672:1344]
        MB = tmp[0:32, 1344:2016]
        CA = tmp[:, 2016:2176]
        CB = tmp[0:32, 2176:2336]
        r336 = tmp[0:32, 2336:2672]
        w336 = tmp[0:32, 2672:3008]
        idx = x3T[:, 1, 512:1024]
        rows = idx[0:32, 0:256]
        win = qT[0:32, 9, 0:320]
        wine = qT[0:32, 8, 0:0 + 320]
        small = sb("small", [128, 160])
        ti = sb("ti", [128, 24], I32)
        blk = sb("blk", [32, 21], I32)
        kvf = small[:, 0:1]
        rf = small[:, 1:2]
        oh = small[0:32, 2:18]
        blkf = small[0:32, 18:39]
        bwA = small[:, 39:40]
        bwB = small[0:32, 40:41]
        tA = small[:, 41:57]
        vA = small[:, 57:73]
        gA = small[:, 73:89]
        tB = small[0:32, 89:105]
        vB = small[0:32, 105:121]
        gB = small[0:32, 121:137]
        VA = small[:, 137:153]
        ones = sb("ones", [32, 128])
        VB = sb("VB", [32, 16])

        ringA = Ring(psum)
        ringS = Ring(psum[0:3])
        ringT = Ring(psum[3:6])
        ringO = Ring([psum[6]])
        ringF = Ring([psum[7]])

        block = ctx.enter_context(nc.Block())

        PAIRS = range(NPAIR)
        HEADS = [(b, g) for b in range(NB) for g in range(4)]

        @block.tensor
        def _(pe):
            def need(*key):
                book.need(pe, "pe", *key)

            def done(ins, *key):
                book.done(ins, "pe", *key)

            mm, tr = nc.tensor.matmul, nc.tensor.transpose

            def layer0(G):
                need("ld", "x", G)
                need("w0", G)
                if G >= 1:
                    need("x2", G - 1, 3)
                for fc in range(4):
                    ps = ringA.take(need, ("x1", G, fc), [("x1c", G, fc)])
                    for p in range(4):
                        ins = mm(ps[:, p * 128:(p + 1) * 128], xs[:, p, fc * 128:(fc + 1) * 128], w0[:, G % 2, p, :],
                                 start=True, stop=True)
                    done(ins, "x1", G, fc)

            def factors():
                need("ld", "wt")
                need("ld", "at")
                ps = ringA.take(need, ("u1",), [("u1c",)])
                for i in range(4):
                    for j in range(4):
                        ins = mm(ps[:, i * 64:(i + 1) * 64], wt[:, j, i * 128:(i + 1) * 128], at[:, j, :],
                                 start=(j == 0), stop=(j == 3))
                done(ins, "u1")
                need("ld", "wp")
                need("ld", "bt")
                ps = ringA.take(need, ("v1",), [("v1c",)])
                for j in range(4):
                    ins = mm(ps[0:64, :], bt[:, j, :], wp[:, j, :], start=(j == 0), stop=(j == 3))
                done(ins, "v1")

            def low(G, s, src, dense, u, z, v, M):
                pre = ("x1c", "x2c")[s - 1]
                ps = ringA.take(need, (f"z{s}", G), [(f"z{s}c", G)])
                for k in range(4):
                    need(pre, G, k)
                    ins = mm(ps[0:M, :], u[:, k, :], src[:, k, :], start=(k == 0), stop=(k == 3))
                done(ins, f"z{s}", G)
                for o in range(4):
                    ps = ringA.take(need, (f"x{s + 1}", G, o), [(f"x{s + 1}c", G, o)])
                    for k in range(4):
                        mm(ps[:, :], dense[:, k, o * 128:(o + 1) * 128], src[:, k, :], start=(k == 0), stop=False)
                    need(f"z{s}c", G)
                    ins = mm(ps[:, :], v[0:M, o * 128:(o + 1) * 128], z[0:M, :], start=False, stop=True)
                    done(ins, f"x{s + 1}", G, o)

            def kv(p):
                G = p // 4
                ps = ringA.take(need, ("kv", p), [("kvv", p), ("ksq", p), ("ky", p)])
                for k in range(4):
                    need("x3c", G, k)
                    ins = mm(ps[:, :], x3T[:, k, p * 128:(p + 1) * 128], wq[:, k, 512:1024], start=(k == 0), stop=(k == 3))
                done(ins, "kv", p)

            def q(p):
                ps = ringA.take(need, ("q", p), [("qsq", p), ("qy", p)])
                for k in range(4):
                    ins = mm(ps[:, :], x3T[:, k, p * 128:(p + 1) * 128], wq[:, k, 0:512], start=(k == 0), stop=(k == 3))
                done(ins, "q", p)

            def qt(p):
                need("qr", p)
                ps = ringA.take(need, ("qt", p), [("qtc", p)])
                for gp in range(2):
                    for h in range(2):
                        o = ps[:, gp * 256:(gp + 1) * 256].rearrange("p (b h t) -> p h b t", b=2, h=2)[:, h]
                        ins = tr(o, qr[:, p % 3, h * 256 + gp * 128:h * 256 + gp * 128 + 128], ident)
                done(ins, "qt", p)

            def index_old():
                need("rows")
                ps = ringA.take(need, ("io",), [("ioc",)])
                for j in range(2):
                    ins = tr(ps[:, j * 32:(j + 1) * 32], rows[:, j * 128:(j + 1) * 128], c("ident", 0, 32)[:, 0:32])
                done(ins, "io")

            def index_spread():
                need("E")
                ps0 = ringA.take(need, ("spA",), [("MA0",), ("MB0",)])
                mm(ps0[:, 0:320], ones[:, :], E[:, 0:10, :], start=True, stop=True)
                ps1 = ringA.take(need, ("spB",), [("MA1",), ("MB1",), ("CA",), ("CB",)])
                mm(ps1[:, 0:352], ones[:, :], E[:, 10:21, :], start=True, stop=True)
                ps = ringA.take(need, ("bw",), [("bwc",), ("bwd",)])
                mm(ps[:, 0:1], E[:, 16:20, :], ones[:, 0:1], start=True, stop=True)
                ins = mm(ps[0:32, 8:9], E[:, 20, :], ones[:, 0:1], start=True, stop=True)
                done(ins, "bw")

            def index_kill():
                need("CA")
                need("CB")
                need("vA")
                need("vB")
                ps = ringA.take(need, ("kill",), [("VA",), ("VB",)])
                mm(ps[:, 0:16], CA[:, 0:128], vA, start=True, stop=False)
                mm(ps[:, 0:16], CB[:, 0:128], vB, start=False, stop=True)
                mm(ps[0:32, 16:32], CA[:, 128:160], vA, start=True, stop=False)
                ins = mm(ps[0:32, 16:32], CB[:, 128:160], vB, start=False, stop=True)
                done(ins, "kill")

            def index_win():
                for k in ("VA", "VB", "MA0", "MB0", "MA1", "MB1"):
                    need(k)
                ps = ringA.take(need, ("win",), [("w336",)])
                for i in range(21):
                    mm(ps[0:32, i * 16:(i + 1) * 16], MA[:, i * 32:(i + 1) * 32], VA, start=True, stop=False)
                    ins = mm(ps[0:32, i * 16:(i + 1) * 16], MB[:, i * 32:(i + 1) * 32], VB[:, :], start=False, stop=True)
                done(ins, "win")

            def index_winT():
                need("wine")
                i32 = c("ident", 0, 32)[:, 0:32]
                ps = ringA.take(need, ("wt",), [("iwc",), ("inwc",), ("inwd",)])
                for j in range(2):
                    tr(ps[:, j * 32:(j + 1) * 32], wine[:, j * 128:(j + 1) * 128], i32)
                ins = tr(ps[0:64, 64:96], wine[:, 256:320], i32)
                done(ins, "wt")

            need("ld", "cf")
            layer0(0)
            factors()
            need("u1c")
            need("d1")
            need("ld", "u2")
            for G in range(NG):
                if G == 0:
                    need("v1c")
                low(G, 1, x1T, d1, u1, z1, v1, 64)
                if G == 0:
                    index_old()
                if G >= 1:
                    for p in range(4 * G - 2, 4 * G):
                        qt(p)
                if G < NG - 1:
                    layer0(G + 1)
                if G == 0:
                    need("d2")
                    need("ld", "v2")
                    index_spread()
                if G == 1:
                    index_winT()
                low(G, 2, x2T, d2, u2, z2, v2, 128)
                if G == 0:
                    need("ld", "wq")
                for p in range(4 * G, 4 * G + 4):
                    kv(p)
                if G == 0:
                    index_kill()
                for p in range(4 * G, 4 * G + 4):
                    q(p)
                    if p % 4 == 2:
                        qt(p - 2)
                    if p % 4 == 3:
                        qt(p - 2)
                if G == 0:
                    index_win()
            qt(14)
            qt(15)

            def keys(b):
                p, h = b // 2, b % 2
                for c_ in range(2):
                    need("old", b, c_)
                    need("patch", b, c_)
                need("new", p)
                for gp in range(2):
                    ps = ringT.take(need, ("kt", b, gp), [("ktc", b, gp)])
                    for c_ in range(2):
                        tr(ps[:, c_ * 128:(c_ + 1) * 128], KVo[:, p % RO, h * 2 + c_, gp * 128:(gp + 1) * 128], ident)
                    hs = slice(h * 64, h * 64 + 64)
                    ins = tr(ps[:, 256:320], KVn[hs, p % 2, gp * 128:(gp + 1) * 128], c("ident", h * 64, h * 64 + 64)[:, hs])
                    done(ins, "kt", b, gp)

            def scores(n):
                b, g = HEADS[n]
                p, h, gp, g2 = b // 2, b % 2, g // 2, g % 2
                need("qtc", p)
                need("ktc", b, gp)
                ps = ringS.take(need, ("s", n), [("sp", n)])
                rr = slice(g2 * 64, g2 * 64 + 64)
                ins = mm(ps[:, 0:320], qT[rr, p, gp * 256 + h * 128:gp * 256 + h * 128 + 128], ks[rr, b % 2, gp, :],
                         start=True, stop=True)
                done(ins, "s", n)

            def turn(n):
                b, g = HEADS[n]
                need("exp", n)
                ps = ringT.take(need, ("pt", n), [("ptc", n)])
                for c_ in range(2):
                    tr(ps[:, c_ * 128:(c_ + 1) * 128], Pp[:, n % 3, c_ * 128:(c_ + 1) * 128], ident)
                a = 256 - 64 * (b % 2)
                ins = tr(ps[:, 256:384], Pp[:, n % 3, a:a + 128], ident)
                done(ins, "pt", n)

            def values(n):
                b, g = HEADS[n]
                p, h = b // 2, b % 2
                if g == 0:
                    ringO.take(need, ("o", b), [("oc", b)])
                ps = ringO.where[("o", b)]
                need("ptc", n)
                o = ps[:, g * 64:(g + 1) * 64]
                for c_ in range(2):
                    mm(o, PT[:, n % 3, c_ * 128:(c_ + 1) * 128], KVo[:, p % RO, h * 2 + c_, 256 + g * 64:320 + g * 64],
                       start=(c_ == 0), stop=False)
                hs = slice(h * 64, h * 64 + 64)
                ins = mm(o, PT[hs, n % 3, 256:384], KVn[hs, p % 2, 256 + g * 64:320 + g * 64], start=False, stop=True)
                done(ins, "pv", n)

            def turn_out(b):
                need("oc", b)
                ps = ringT.take(need, ("ot", b), [("otc", b)])
                for gp in range(2):
                    ins = tr(ps[:, gp * 128:(gp + 1) * 128], Os[:, b % 2, gp * 128:(gp + 1) * 128], ident)
                done(ins, "ot", b)

            def final(p):
                need("ld", "wo")
                ps = ringF.take(need, ("f", p), [("fc", p)])
                for k in range(4):
                    mm(ps[:, k * 128:(k + 1) * 128], x3T[:, k, p * 128:(p + 1) * 128], ident, is_transpose=True,
                       start=(k == 0), stop=False, skip_group_check=True)
                need("otc", 2 * p)
                need("otc", 2 * p + 1)
                for k in range(4):
                    ins = mm(ps[:, :], oT[:, p % 2, k // 2, k % 2, :], wo[:, k, :], start=False, stop=(k == 3),
                             skip_group_check=True)
                done(ins, "f", p)

            for r in ringA.readers:
                for k in r:
                    need(*k)
            keys(0)
            for n in range(128 + 9):
                if n % 4 == 1 and n // 4 + 1 < NB:
                    keys(n // 4 + 1)
                if n < 128:
                    scores(n)
                if 0 <= n - 2 < 128:
                    turn(n - 2)
                if 0 <= n - 3 < 128:
                    values(n - 3)
                if n >= 8 and n % 4 == 0 and n // 4 - 2 < NB:
                    turn_out(n // 4 - 2)
                if n >= 13 and n % 8 == 5 and (n - 13) // 8 < NPAIR:
                    final((n - 13) // 8)
            final(15) if ("f", 15) not in book.new else None

        @block.scalar
        def _(act):
            def need(*key):
                book.need(act, "act", *key)

            def done(ins, *key):
                book.done(ins, "act", *key)

            need("ang")
            for n in range(2):
                ins = nc.scalar.activation((t1, t2)[n][:, :], (sq, yy)[n][:, :], ACT.Sin)
            done(ins, "sincos")

            def x1c(G):
                if G >= 1:
                    need("x2", G - 1, 3)
                for fc in range(4):
                    need("x1", G, fc)
                    done(nc.scalar.copy(x1T[:, fc, :], ringA.where[("x1", G, fc)][:, :]), "x1c", G, fc)

            x1c(0)
            need("u1")
            done(nc.scalar.copy(u1[:, :, :].rearrange("p a b -> p (a b)"), ringA.where[("u1",)][:, 0:256]), "u1c")
            for G in range(NG):
                for o in (0, 2):
                    if G >= 1:
                        need("x3", G - 1, 3)
                    need("x2", G, o)
                    done(nc.scalar.copy(x2T[:, o, :], ringA.where[("x2", G, o)][:, :]), "x2c", G, o)
                if G >= 1:
                    for p in range(4 * G - 2, 4 * G):
                        need("qt", p)
                        done(nc.scalar.copy(qT[:, p, :], ringA.where[("qt", p)][:, :]), "qtc", p)
                if G < NG - 1:
                    x1c(G + 1)
                for o in (0, 2):
                    need("x3", G, o)
                    done(nc.scalar.copy(x3T[:, o, G * 512:(G + 1) * 512], ringA.where[("x3", G, o)][:, :]), "x3c", G, o)

                def square(kind, p, w):
                    need(kind, p)
                    if kind == "kv":
                        if p >= 2:
                            need("ld", "n", p - 2)
                        done(nc.scalar.copy(nt[:, p % 2, 256:512], ringA.where[("kv", p)][:, 256:512]), "kvv", p)
                        if p >= 1:
                            need("kss", p - 1) if p % 4 else need("qss", p - 1)
                    else:
                        need("kss", p + 3) if p % 4 == 0 else need("qss", p - 1)
                    done(nc.scalar.square(sq[:, 0:w], ringA.where[(kind, p)][:, 0:w]), kind[0] + "sq", p)
                    need(kind[0] + "s1", p)
                    r = ss[:, 0 if kind == "kv" else 1, 0:w // 64]
                    done(nc.scalar.sqrt(r, r), kind[0] + "root", p)
                need("tab")
                for p in range(4 * G, 4 * G + 4):
                    square("kv", p, 256)
                for p in range(4 * G, 4 * G + 4):
                    square("q", p, 512)
                    if p % 4 >= 2:
                        need("qt", p - 2)
                        if p - 2 >= 8:
                            need("iwc")
                        done(nc.scalar.copy(qT[:, p - 2, :], ringA.where[("qt", p - 2)][:, :]), "qtc", p - 2)
            for p in (14, 15):
                need("qt", p)
                done(nc.scalar.copy(qT[:, p, :], ringA.where[("qt", p)][:, :]), "qtc", p)

            def ktc(b):
                need("x3", 3, 3)
                need("kt", b, 0)
                if b >= 2:
                    need("s", 4 * (b - 2) + 1)
                done(nc.scalar.copy(ks[:, b % 2, 0, :], ringT.where[("kt", b, 0)][:, 0:320]), "ktc", b, 0)

            ktc(0)
            for n in range(128 + 12):
                if n % 4 == 1 and n // 4 + 1 < NB:
                    ktc(n // 4 + 1)
                if n < 128:
                    need("sp", n)
                    need("pzero")
                    if n >= 3:
                        need("pt", n - 3)
                    done(nc.scalar.activation(Pp[:, n % 3, 0:320], Sp[:, n % 3, :], ACT.Exp, bias=nmx[:, n:n + 1],
                                              scale=-1.0, accum_out=sm[:, n:n + 1]), "exp", n)
                m = n - 2
                if 0 <= m < 128 and m % 2 == 0:
                    need("pt", m)
                    if m >= 3:
                        need("pv", m - 3)
                    done(nc.scalar.copy(PT[:, m % 3, :], ringT.where[("pt", m)][:, 0:384]), "ptc", m)
                if n >= 13 and n % 8 == 5 and (n - 13) // 8 < NPAIR:
                    p = (n - 13) // 8
                    need("f", p)
                    if p >= 2:
                        need("ld", "out", p - 2)
                    done(nc.scalar.copy(Fo[:, p % 2, :], ringF.where[("f", p)][:, :]), "fc", p)

        @block.vector
        def _(dve):
            def need(*key):
                book.need(dve, "dve", *key)

            def done(ins, *key):
                book.done(ins, "dve", *key)
                return key

            v = nc.vector

            def step(ins, *key):
                done(ins, *key)
                need(*key)

            need("ld", "cf")
            need("ld", "ci")
            need("ld", "fs")
            done(v.tensor_scalar(w0i[:, :], cint("cond"), 64, None, ALU.mult), "w0i0")
            step(v.tensor_scalar(ti[:, 0:1], cint("kvw"), 4, None, ALU.arith_shift_right), "ti0")
            done(v.tensor_scalar(ti[:, 1:2], cint("kvw"), 15, None, ALU.bitwise_and), "ti1")
            done(v.tensor_tensor(w0i[:, :], w0i[:, :], cint("c").to_broadcast([128, 16]), ALU.add), "w0i")
            done(v.tensor_tensor(ti[:, 2:3], ti[:, 0:1], cint("b257"), ALU.add), "ti")
            done(v.memset(w0[:, :, :, :], 0.0), "w0z")
            done(v.memset(ones[:, :], 1.0), "ones")
            need("ti1")
            step(v.tensor_copy(rf, ti[:, 1:2]), "rf")
            step(v.tensor_scalar(oh, c("iota16", 0, 32), rf[0:32, :], None, ALU.is_equal), "oh")
            done(v.tensor_scalar(mk1[:, :], cint("idx1", 0, 64), c("e", 0, 64), None, ALU.is_equal), "mk1")
            done(v.tensor_scalar(mk2[:, :], cint("idx2"), c("e"), None, ALU.is_equal), "mk2")
            done(v.tensor_scalar(thr[:, :], cint("kvall"), -256.0, BIGC, ALU.add, ALU.mult), "thr")
            need("w0z")

            def blockdiag(G):
                need("ld", "stage", G)
                if G >= 2:
                    need("x1", G - 2, 3)
                for h in range(2):
                    a = slice(h * 64, h * 64 + 64)
                    idb = c("ident", h * 64, h * 64 + 64)[:, a]
                    ins = v.tensor_tensor(w0[a, G % 2, :, a], stage[a, 4 * G:4 * G + 4, :],
                                          idb.unsqueeze(1).to_broadcast([64, 4, 64]), ALU.add)
                done(ins, "w0", G)

            ang = t1[:, :].rearrange("p (a d) -> p a d", a=16)
            kvt = small[:, 2:18]
            kvg = t2[:, 0:16]
            step(v.tensor_copy(kvg, cint("kvtok")), "kvg0")
            step(v.tensor_scalar(kvg, kvg, c("t"), None, ALU.add), "kvg")
            step(v.tensor_tensor(ang, kvg.unsqueeze(2).to_broadcast([128, 16, 32]),
                                 c("inv").unsqueeze(1).to_broadcast([128, 16, 32]), ALU.mult), "ang0")
            A = t1[:, :]
            n_, m_ = idx[:, :], t2[:, :]
            for i, (dst, off) in enumerate(((sq[:, :], 0.0), (yy[:, :], 0.25))):
                step(v.tensor_scalar(n_, A, float(1.0 / TWO_PI), off, ALU.mult, ALU.add), "rr", i, 0)
                step(v.tensor_scalar(m_, n_, MAGIC, None, ALU.add), "rr", i, 1)
                step(v.tensor_scalar(n_, m_, -MAGIC, None, ALU.add), "rr", i, 2)
                step(v.scalar_tensor_tensor(dst, n_, -C1, A, ALU.mult, ALU.add), "rr", i, 3)
                step(v.scalar_tensor_tensor(m_, n_, -C2, dst, ALU.mult, ALU.add), "rr", i, 4)
                step(v.scalar_tensor_tensor(dst, n_, -C3, m_, ALU.mult, ALU.add), "rr", i, 5)
                if off:
                    step(v.tensor_scalar(dst, dst, float(np.pi / 2), None, ALU.add), "rr", i, 6)
                step(v.tensor_scalar(dst, dst, 3.1415925, -3.1415925, ALU.min, ALU.max), "rr", i, 7)
            done(v.tensor_copy(gg[:, 0, 0, 0:1], dst[:, 0:1]), "ang")
            need("ang")
            blockdiag(0)
            for n, nm in enumerate(("qs", "ks")):
                s2 = f(nm).rearrange("p (a b) -> p a b", a=2)
                v.tensor_scalar(gg[:, 2 * n, :, :], s2, 1.0, 8.0, ALU.add, ALU.mult)
                v.tensor_scalar(gg[:, 2 * n + 1, 0, :], s2[:, 1, :], 1.0, -8.0, ALU.add, ALU.mult)
                ins = v.tensor_scalar(gg[:, 2 * n + 1, 1, :], s2[:, 0, :], 1.0, 8.0, ALU.add, ALU.mult)
            done(ins, "gg")
            need("ld", "blk")
            step(v.tensor_copy(blkf, blk[:, :]), "blkf")
            step(v.scalar_tensor_tensor(r336.rearrange("p (i o) -> p i o", o=16),
                                        blkf.unsqueeze(2).to_broadcast([32, 21, 16]), 16.0,
                                        c("iota16", 0, 32).unsqueeze(1).to_broadcast([32, 21, 16]), ALU.mult, ALU.add), "r336")
            done(v.tensor_tensor(E, blkf.unsqueeze(2).to_broadcast([32, 21, 32]),
                                 c("ident", 0, 32)[:, 0:32].unsqueeze(1).to_broadcast([32, 21, 32]), ALU.mult), "E")
            step(v.tensor_scalar(rows, r336[:, 0:256], oh[:, 0:1], None, ALU.mult), "rows", 0)
            for k in range(1, 16):
                step(v.scalar_tensor_tensor(rows, r336[:, k:k + 256], oh[:, k:k + 1], rows, ALU.mult, ALU.add), "rows", k)
            done(v.tensor_copy(kvf, rf), "rows")
            need("v1")
            done(v.tensor_scalar(v1[:, :], ringA.where[("v1",)][0:64, :], f("s1", 0, 64), None, ALU.mult), "v1c")
            need("ld", "d1")
            for k in range(4):
                o = d1[:, k, k * 128:(k + 1) * 128]
                ins = v.tensor_tensor(o, o, ident, ALU.add)
            done(ins, "d1")
            for nm, P, t_, v_, g_, m16, val in (("A", 128, tA, vA, gA, "m16", "val"), ("B", 32, tB, vB, gB, "m16b", "valb")):
                step(v.tensor_scalar(t_, c("iota16", 0, P), c(m16, 0, P), rf[0:P, :], ALU.add, ALU.subtract), "t", nm)
                v.tensor_scalar(v_, t_, 0.0, None, ALU.is_ge)
                step(v.tensor_scalar(g_, t_, 63.0, None, ALU.is_le), "le", nm)
                step(v.tensor_tensor(v_, v_, g_, ALU.mult), "v" + nm)
                step(v.tensor_scalar(g_, t_, c(val, 0, P), None, ALU.add), "g", nm)

            need("sincos")
            need("gg")
            sin = t1[:, :].rearrange("p (a d) -> p a d", a=16).unsqueeze(2).to_broadcast([128, 16, 2, 32])
            cos = t2[:, :].rearrange("p (a d) -> p a d", a=16).unsqueeze(2).to_broadcast([128, 16, 2, 32])
            for n, nm in enumerate("qk"):
                v.tensor_tensor(tab[nm, "a"][:, :, :, :], cos, gg[:, 2 * n, :, :].unsqueeze(1).to_broadcast([128, 16, 2, 32]),
                                ALU.mult)
                ins = v.tensor_tensor(tab[nm, "b"][:, :, :, :], sin,
                                      gg[:, 2 * n + 1, :, :].unsqueeze(1).to_broadcast([128, 16, 2, 32]), ALU.mult)
            done(ins, "tab")
            need("tab")

            def match():
                need("bw")
                v.tensor_copy(bwA, ringA.where[("bw",)][:, 0:1])
                done(v.tensor_copy(bwB, ringA.where[("bw",)][0:32, 8:9]), "bwc")
                need("bwc")
                book.new[("bwd",)] = book.new[("bwc",)]
                a, b_ = ringA.where[("spA",)], ringA.where[("spB",)]
                done(v.tensor_scalar(MA[:, 0:320], a[:, 0:320], bwA, None, ALU.is_equal), "MA0")
                done(v.tensor_scalar(MA[:, 320:672], b_[:, 0:352], bwA, None, ALU.is_equal), "MA1")
                done(v.tensor_scalar(MB[:, 0:320], a[0:32, 0:320], bwB, None, ALU.is_equal), "MB0")
                done(v.tensor_scalar(MB[:, 320:672], b_[0:32, 0:352], bwB, None, ALU.is_equal), "MB1")
                done(v.scalar_tensor_tensor(CA, b_[:, 192:352], bwA, c("la"), ALU.is_equal, ALU.mult), "CA")
                done(v.scalar_tensor_tensor(CB, b_[0:32, 192:352], bwB, c("lb", 0, 32), ALU.is_equal, ALU.mult), "CB")

            def survive():
                need("kill")
                ps = ringA.where[("kill",)]
                for nm, P, o, t_, v_, g_, V in (("A", 128, 0, tA, vA, gA, VA), ("B", 32, 16, tB, vB, gB, VB[:, :])):
                    step(v.tensor_scalar(t_, ps[0:P, o:o + 16], 0.0, None, ALU.is_equal), "alive", nm)
                    step(v.tensor_tensor(t_, t_, v_, ALU.mult), "alive2", nm)
                    done(v.tensor_tensor(V, t_, g_, ALU.mult), "V" + nm)

            def winners():
                need("win")
                step(v.tensor_copy(w336, ringA.where[("win",)][0:32, 0:336]), "w336")
                step(v.tensor_scalar(win, w336[:, 0:320], oh[:, 0:1], None, ALU.mult), "winner", 0)
                for k in range(1, 16):
                    w = min(320, 336 - k)
                    step(v.scalar_tensor_tensor(win[:, 0:w], w336[:, k:k + w], oh[:, k:k + 1], win[:, 0:w], ALU.mult,
                                                ALU.add), "winner", k)
                step(v.tensor_scalar(wine, win, 0.0, SKIP, ALU.is_equal, ALU.mult), "wine0")
                step(v.scalar_tensor_tensor(wine, win, -1.0, wine, ALU.add, ALU.add), "wine")

            def indices():
                need("wt")
                ps = ringA.where[("wt",)]
                done(v.tensor_copy(iw[:, :, :].rearrange("p a b -> p (a b)"), ps[:, 0:64]), "iwc")
                pr = ps[0:64, 64:96].rearrange("p (a b) -> p b a", b=2)
                done(v.tensor_copy(inw[0:64, :], pr[:, 0, :]), "inwc")
                done(v.tensor_copy(inw[64:128, :], pr[:, 1, :]), "inwd")

            def zc(G, s, z, mk, M):
                need(f"z{s}", G)
                need("mk1")
                need("mk2")
                if G >= 1:
                    need(f"x{s + 1}", G - 1, 3)
                done(v.tensor_tensor(z[0:M, :].rearrange("p (b t) -> p b t", b=8),
                                     ringA.where[(f"z{s}", G)][0:M, :].rearrange("p (b t) -> p b t", b=8),
                                     mk[0:M, 8 * G:8 * G + 8].unsqueeze(2).to_broadcast([M, 8, 64]), ALU.mult), f"z{s}c", G)

            def rope(kind, p, nh, dst):
                w = nh * 64
                k0 = kind[0]
                r = ss[:, 0 if k0 == "k" else 1, 0:nh]
                need(k0 + "sq", p)
                step(v.tensor_reduce(r, sq[:, 0:w].rearrange("p (h d) -> p h d", d=64), AX.X, ALU.add), k0 + "ss", p)
                done(v.tensor_scalar(r, r, 64e-6, None, ALU.add), k0 + "s1", p)
                need(k0 + "root", p)
                step(v.reciprocal(r, r), k0 + "s2", p)
                y = yy[:, 0:w].rearrange("p (h a d) -> p h a d", a=2, d=32)
                step(v.tensor_tensor(yy[:, 0:w].rearrange("p (h d) -> p h d", d=64),
                                     ringA.where[(kind, p)][:, 0:w].rearrange("p (h d) -> p h d", d=64),
                                     r.unsqueeze(2).to_broadcast([128, nh, 64]), ALU.mult), k0 + "y", p)
                a, b_ = tab[k0, "a"][:, p, :, :], tab[k0, "b"][:, p, :, :]
                v.tensor_tensor(t1[:, 0:w].rearrange("p (h a d) -> p h a d", a=2, d=32), y,
                                a.unsqueeze(1).to_broadcast([128, nh, 2, 32]), ALU.mult)
                t2v = t2[:, 0:w].rearrange("p (h a d) -> p h a d", a=2, d=32)
                for a_ in range(2):
                    ins = v.tensor_tensor(t2v[:, :, a_, :], y[:, :, 1 - a_, :],
                                          b_[:, a_, :].unsqueeze(1).to_broadcast([128, nh, 32]), ALU.mult)
                step(ins, k0 + "sum", p)
                return done(v.tensor_tensor(dst, t1[:, 0:w], t2[:, 0:w], ALU.add), {"k": "kr", "q": "qr"}[k0], p)

            need("ioc") if False else None
            for G in range(NG):
                if G + 1 < NG:
                    blockdiag(G + 1) if G == 0 else None
                zc(G, 1, z1, mk1, 64)
                for o in (1, 3):
                    need("x2", G, o)
                    if G >= 1:
                        need("x3", G - 1, 3)
                    done(v.tensor_copy(x2T[:, o, :], ringA.where[("x2", G, o)][:, :]), "x2c", G, o)
                if G == 0:
                    need("io")
                    done(v.tensor_copy(io[:, :, :].rearrange("p a b -> p (a b)"), ringA.where[("io",)][:, 0:64]), "ioc")
                    need("ld", "d2")
                    for k in range(4):
                        o = d2[:, k, k * 128:(k + 1) * 128]
                        ins = v.tensor_tensor(o, o, ident, ALU.add)
                    done(ins, "d2")
                    need("ld", "v2")
                    done(v.tensor_scalar(v2[:, :], v2[:, :], f("s2"), None, ALU.mult), "v2")
                    match()
                    blockdiag(2)
                    blockdiag(3)
                    winners_after = True
                if G == 1:
                    indices()
                zc(G, 2, z2, mk2, 128)
                for o in (1, 3):
                    need("x3", G, o)
                    done(v.tensor_copy(x3T[:, o, G * 512:(G + 1) * 512], ringA.where[("x3", G, o)][:, :]), "x3c", G, o)
                for p in range(4 * G, 4 * G + 4):
                    if p >= 2:
                        need("ld", "n", p - 2)
                    rope("kv", p, 4, nt[:, p % 2, 0:256])
                if G == 0:
                    survive()
                for p in range(4 * G, 4 * G + 4):
                    if p >= 3:
                        need("qt", p - 3)
                    rope("q", p, 8, qr[:, p % 3, :])
                if G == 0:
                    winners()

            need("x3", 3, 3)
            for r in range(3):
                ins = v.memset(Pp[:, r, 320:384], 0.0)
            done(ins, "pzero")
            for r in range(2):
                ins = v.tensor_copy(mask[:, r, 256:320], c("band")[:, 256:320])
            done(ins, "mask0")

            def maskb(b):
                done(v.scalar_tensor_tensor(mask[:, b % 2, 0:256], c("iotac"), thr[:, b:b + 1], c("band")[:, 0:256],
                                            ALU.add, ALU.min), "mask", b)

            def ktc(b):
                need("kt", b, 1)
                if b >= 2:
                    need("s", 4 * (b - 2) + 3)
                done(v.tensor_copy(ks[:, b % 2, 1, :], ringT.where[("kt", b, 1)][:, 0:320]), "ktc", b, 1)

            maskb(0)
            ktc(0)
            for n in range(128 + 9):
                if n % 4 == 1 and n // 4 + 1 < NB:
                    ktc(n // 4 + 1)
                    maskb(n // 4 + 1)
                if n < 128:
                    b = n // 4
                    need("s", n)
                    need("mask", b)
                    need("mask0")
                    if n >= 3:
                        need("exp", n - 3)
                    done(v.tensor_tensor_reduce(Sp[:, n % 3, :], ringS.where[("s", n)][:, 0:320], mask[:, b % 2, :],
                                                -0.0625, 3.0e38, ALU.add, ALU.min, nmx[:, n:n + 1]), "sp", n)
                m = n - 2
                if 0 <= m < 128 and m % 2 == 1:
                    need("pt", m)
                    if m >= 3:
                        need("pv", m - 3)
                    done(v.tensor_copy(PT[:, m % 3, :], ringT.where[("pt", m)][:, 0:384]), "ptc", m)
                m = n - 3
                if 0 <= m < 128 and m % 4 == 3:
                    b = m // 4
                    need("exp", m)
                    step(v.reciprocal(rs[:, 4 * b:4 * b + 4], sm[:, 4 * b:4 * b + 4]), "rs", b)
                    need("pv", m)
                    if b >= 2:
                        need("ot", b - 2)
                    done(v.tensor_tensor(Os[:, b % 2, :].rearrange("p (g d) -> p g d", g=4),
                                         ringO.where[("o", b)][:, 0:256].rearrange("p (g d) -> p g d", g=4),
                                         rs[:, 4 * b:4 * b + 4].unsqueeze(2).to_broadcast([128, 4, 64]), ALU.mult), "oc", b)
                if n >= 8 and n % 4 == 0 and n // 4 - 2 < NB:
                    b = n // 4 - 2
                    need("ot", b)
                    if b >= 4:
                        need("f", b // 2 - 2)
                    h = b % 2
                    for gp in range(2):
                        ins = v.tensor_copy(oT[:, (b // 2) % 2, gp, :, h * 64:h * 64 + 64],
                                            ringT.where[("ot", b)][:, gp * 128:(gp + 1) * 128].rearrange("p (h t) -> p h t", h=2))
                    done(ins, "otc", b)

        @block.gpsimd
        def _(pool):
            def need(*key):
                book.need(pool, "pool", *key)

            off = bass.IndirectOffsetOnAxis

            need("ti")
            book.done(nc.gpsimd.indirect_dma_start(blk[:, :], None, TBL[:, :], off(ap=ti[0:32, 2:3].bitcast(U32), axis=0)),
                      "g_blk", "ld", "blk")
            need("w0i")
            for G in range(4):
                for p in range(4 * G, 4 * G + 4):
                    ins = nc.gpsimd.indirect_dma_start(stage[:, p, :], None, W0[:, :],
                                                       off(ap=w0i[:, p:p + 1].bitcast(U32), axis=0))
                    book.done(ins, f"g_w{G}", "stage", p)
                book.new[("ld", "stage", G)] = book.new[("stage", 4 * G + 3)]

            def old(p):
                if p >= RO:
                    need("pv", 8 * (p - RO) + 7)
                for h in range(2):
                    for c_ in range(2):
                        b = 2 * p + h
                        ins = nc.gpsimd.indirect_dma_start(KVo[:, p % RO, h * 2 + c_, :], None, KV[:, :],
                                                           off(ap=io[:, c_, b:b + 1], axis=0))
                        book.done(ins, f"g_o{(p % RO)}_{h}{c_}", "old", b, c_)

            need("ioc")
            for p in range(RO):
                if p == RO - 1:
                    need("x1", 3, 3)
                    need("z2", 3)
                old(p)
            need("iwc")
            need("inwc")
            need("inwd")
            for p in PAIRS:
                need("ld", "n", p)
            for p in PAIRS:
                if p >= 2:
                    need("pv", 8 * (p - 2) + 7)
                ins = nc.gpsimd.indirect_dma_start(KVn[:, p % 2, :], None, SCR[:, :], off(ap=inw[:, p:p + 1], axis=0))
                book.done(ins, f"g_n{p % 2}", "new", p)
                for h in range(2):
                    for c_ in range(2):
                        b = 2 * p + h
                        need("old", b, c_)
                        ins = nc.gpsimd.indirect_dma_start(KVo[:, p % RO, h * 2 + c_, :], None, SCR[:, :],
                                                           off(ap=iw[:, c_, b:b + 1], axis=0),
                                                           bounds_check=2047, oob_is_err=False)
                        book.done(ins, f"g_p{(p % 2)}_{h}{c_}", "patch", b, c_)
                if p >= 1 and p - 1 + RO < NPAIR:
                    old(p - 1 + RO)

        @block.sync
        def _(sp):
            def need(*key):
                book.need(sp, "sp", *key)

            def load(dst, src, *key):
                book.done(nc.sync.dma_start(dst, src), "d_" + "_".join(map(str, key)), "ld", *key)

            load(cf[:, :], CFD[:, :], "cf")
            load(ci[:, :], CID[:, :], "ci")
            load(fs[:, :], FSD[:, :], "fs")
            load(xs, X[:, 0, :, :], "x", 0)
            load(wt, WT[:, :, :], "wt")
            load(at[:, :, :], AT[:, :, :], "at")
            load(wp, WP[:, :, :], "wp")
            load(bt[:, :, :], BT[:, :, :], "bt")
            load(d1, WB[:, :, :], "d1")
            load(u2[:, :, :], A2[:, :, :], "u2")
            load(v2[:, :], V2D[:, :], "v2")
            load(d2, W2[:, :, :], "d2")
            load(wq[:, :, :], WQKV[:, :, :], "wq")
            for G in range(NG):
                if G + 1 < NG:
                    need("x1", G, 3)
                    load(xs, X[:, G + 1, :, :], "x", G + 1)
                for p in range(4 * G, 4 * G + 4):
                    need("kr", p)
                    need("kvv", p)
                    load(SCR[p * 128:(p + 1) * 128, :], nt[:, p % 2, :], "n", p)
            need("q", 15)
            load(wo, WO[:, :, :], "wo")
            for p in PAIRS:
                need("fc", p)
                load(out[p * 128:(p + 1) * 128, :], Fo[:, p % 2, :], "out", p)
            for p in PAIRS:
                need("ld", "out", p)


def _constants():
    cf = np.zeros((128, NCF), np.float32)
    ci = np.zeros((128, 2), np.int32)
    p = np.arange(128)

    def put(name, a):
        lo, hi = CF[name]
        cf[:a.shape[0], lo:hi] = a.reshape(a.shape[0], hi - lo)
    put("ident", np.eye(128, dtype=np.float32))
    t, s = (p % 64)[:, None], np.arange(320)[None, :]
    put("band", np.where((s > t) & (s <= t + 256), 0.0, -1e30))
    put("iotac", np.broadcast_to(np.arange(256) * BIGC, (128, 256)))
    m, b = np.divmod(np.arange(160), 32)
    order = b * 5 + m
    later = (order[:, None] > order[None, :]).astype(np.float32)
    put("la", later[:128])
    put("lb", later[128:])
    put("iota16", np.broadcast_to(np.arange(16.0), (128, 16)))
    half = np.float32(10000.0) ** (np.arange(32, dtype=np.float32) / np.float32(32))
    put("inv", np.broadcast_to((np.float32(1.0) / half).astype(np.float32), (128, 32)))
    put("t", (p % 64).astype(np.float32))
    put("e", (p // 16).astype(np.float32))
    put("m16", (p // 32 * 16.0))
    put("val", (p % 32 * 64.0 + 1))
    put("m16b", np.full(128, 64.0))
    put("valb", (p % 32 * 64.0 + 1))
    ci[:, 0] = p % 64
    ci[:, 1] = p * 257
    return cf, ci


def _layout(i):
    a = {k: np.asarray(v) for k, v in i.items()}
    cf, cc = _constants()
    cond, i1, i2, kv = (a[k].astype(np.int32) for k in ("itok_B_1_198", "itok_B_0_3", "itok_B_0_6", "itok_B_37_3939"))
    ci = np.zeros((128, NCI), np.int32)

    def put(name, v):
        lo, hi = CI[name]
        ci[:, lo:hi] = v

    def by_pair(v):
        return np.repeat(v.reshape(16, 2).T, 64, axis=0)
    put("cond", by_pair(cond))
    put("kvtok", by_pair(kv))
    put("idx1", i1[None, :])
    put("idx2", i2[None, :])
    put("kvall", kv[None, :])
    put("kvw", np.tile(kv, 4)[:, None])
    put("c", cc[:, 0:1])
    put("b257", cc[:, 1:2])
    fs = np.zeros((128, NFS), np.float32)
    fs[:, FS["qs"][0]:FS["qs"][1]] = a["L3_cond_q_norm_scale"][None, :]
    fs[:, FS["ks"][0]:FS["ks"][1]] = a["L3_cond_k_norm_scale"][None, :]
    fs[0:64, FS["s1"][0]] = np.repeat(a["L1_cond_scaling"], 16)
    fs[:, FS["s2"][0]] = np.repeat(a["L2_cond_scalings"], 16)

    def rows(w):
        return np.ascontiguousarray(w.reshape(4, 128, -1).transpose(1, 0, 2))
    tbl = a["itok_Bx257_0_4111"].astype(np.int32)
    at = np.clip(np.arange(257)[:, None] - 16 + np.arange(21)[None, :], 0, 256)
    tbl = np.ascontiguousarray(tbl[:, at].reshape(NB * 257, 21))
    Wq = a["L3_cond_Wq"].reshape(4, 2, 64, 512).transpose(1, 0, 2, 3).reshape(512, 512)
    wqkv = np.concatenate([Wq, a["L3_cond_Wk"], a["L3_cond_Wv"]], 0).T
    wo = a["L3_cond_Wo"].T.reshape(2, 2, 2, 64, 512).transpose(0, 2, 1, 3, 4).reshape(512, 512)
    kvr = np.empty((4112, 16, 2, 4, 64), np.float32)
    kvr[:, :, 0] = a["L3_cond_k_blocks"].transpose(0, 2, 1, 3)
    kvr[:, :, 1] = a["L3_cond_v_blocks"].transpose(0, 2, 1, 3)
    return {
        "X": np.ascontiguousarray(a["x"].reshape(4, 4, 128, 512).transpose(2, 0, 1, 3)),
        "W0": np.ascontiguousarray(a["L0_cond_weights"].reshape(12800, 64)),
        "WB": rows(a["L1_cond_W_base"].T),
        "WT": rows(a["L1_cond_Wt"]),
        "AT": rows(a["L1_cond_A"].reshape(64, 512).T),
        "BT": rows(a["L1_cond_B_w"].transpose(1, 0, 2).reshape(512, 64)),
        "WP": rows(a["L1_cond_Wp"].T),
        "W2": rows(a["L2_cond_W"].T),
        "A2": rows(a["L2_cond_A"].reshape(128, 512).T),
        "V2D": np.ascontiguousarray(a["L2_cond_Bm"].transpose(0, 2, 1).reshape(128, 512)),
        "WQKV": rows(wqkv),
        "WO": rows(wo),
        "KV": kvr.reshape(KVROWS, 512),
        "TBL": tbl,
        "CFD": cf,
        "CID": ci,
        "FSD": fs,
    }


def _build(make, arrays):
    known = None
    for _ in range(2):
        nc = make()
        args = {}
        for name, v in arrays.items():
            args[name] = nc.dram_tensor(f"in_{name}", v.shape, mybir.dt.from_np(v.dtype), kind="ExternalInput").ap()
        args["SCR"] = nc.dram_tensor("scratch", (2048, 512), F32, kind="Internal").ap()
        args["out"] = nc.dram_tensor("out_0_dram", (2048, 512), F32, kind="ExternalOutput").ap()
        book = Book(known)
        program(nc, book, **args)
        known = book.new
    return nc


def kernel(**inputs):
    import concourse.bacc as _bacc
    from concourse.bass_utils import run_bass_kernel_spmd as _run

    arrays = _layout(inputs)
    nc = _build(lambda: _bacc.Bacc("TRN2", target_bir_lowering=False, num_devices=1), arrays)
    r = _run(nc, [{f"in_{k}": v for k, v in arrays.items()}], core_ids=[0])
    return r.results[0]["out_0_dram"].reshape(NB, T, D)
```

```python
from contextlib import ExitStack

import numpy as np

import concourse.bass as bass
from concourse import mybir

F32 = mybir.dt.float32
I32 = mybir.dt.int32
U32 = mybir.dt.uint32
ALU = mybir.AluOpType
ACT = mybir.ActivationFunctionType
AX = mybir.AxisListType

NB, T, D, HD = 32, 64, 512, 64
NPAIR = 16
NG = 4
NBLK = 257
KVROWS = 4112 * 16
RO = 4
RQ = 3
RS, RP, RT = 3, 4, 3
LT, LV, LO, LF = 3, 5, 10, 11
SKIP = 65536.0
BIGC = float(2.0 ** 100)
MAGIC = 12582912.0
TWO_PI = 2.0 * np.pi
C1 = 6.28125
C2 = float(np.float32(np.round((TWO_PI - C1) * 2.0 ** 20) / 2.0 ** 20))
C3 = float(np.float32(TWO_PI - C1 - C2))

CF = {}
CI = {}


def _columns(table, widths):
    at = 0
    for name, w in widths:
        table[name] = (at, at + w)
        at += w
    return at


NCF = _columns(CF, [("ident", 128), ("band", 320), ("iotac", 256), ("la", 160), ("lb", 160), ("iota16", 16),
                    ("inv", 32), ("t", 1), ("e", 1), ("m16", 1), ("val", 1), ("m16b", 1), ("valb", 1)])
NCI = _columns(CI, [("cond", 16), ("kvtok", 16), ("idx1", 32), ("idx2", 32), ("kvall", 32), ("kvw", 1),
                    ("c", 1), ("b257", 1)])
FS = {}
NFS = _columns(FS, [("qs", 64), ("ks", 64), ("s1", 1), ("s2", 1)])


class Book:

    def __init__(self, known):
        self.known, self.new, self.count, self.seen, self.sem = known, {}, {}, {}, {}

    def start(self, nc, ctx):
        self.nc, self.ctx = nc, ctx

    def _sem(self, s):
        if s not in self.sem:
            self.sem[s] = self.ctx.enter_context(self.nc.semaphore("s_" + s))
        return self.sem[s]

    def done(self, ins, s, *key):
        n = 1 if s in ("pe", "act", "dve", "pool") else 16
        self.count[s] = self.count.get(s, 0) + n
        ins.then_inc(self._sem(s), n)
        assert key not in self.new, key
        self.new[key] = (s, self.count[s])

    def need(self, eng, who, *key):
        s, v = self.known.get(key, ("pe", 0)) if self.known is not None else ("pe", 0)
        if self.known and key not in self.known:
            raise KeyError(key)
        if self.seen.get((who, s), 0) < v:
            self.seen[(who, s)] = v
            eng.wait_ge(self._sem(s), v)


class Ring:

    def __init__(self, banks):
        self.banks, self.n, self.readers, self.where = banks, 0, [()] * len(banks), {}

    def take(self, need, key, readers):
        i = self.n % len(self.banks)
        self.n += 1
        for r in self.readers[i]:
            need(*r)
        self.readers[i] = readers
        self.where[key] = self.banks[i]
        return self.banks[i]


def program(nc, book, X, W0, WB, WT, AT, BT, WP, W2, A2, V2D, WQKV, WO, KV, TBL, CFD, CID, FSD, SCR, out):
    ctx = ExitStack()
    with ctx:
        book.start(nc, ctx)

        def sb(name, shape, dt=F32):
            return ctx.enter_context(nc.sbuf_tensor(name, shape, dt))

        psum = [ctx.enter_context(nc.psum_tensor(f"ps{i}", [128, 512], F32)) for i in range(8)]

        cf = sb("cf", [128, NCF])
        ci = sb("ci", [128, NCI], I32)
        fs = sb("fs", [128, NFS])

        def c(name, p0=0, p1=128):
            a, b = CF[name]
            return cf[p0:p1, a:b]

        def cint(name, p0=0, p1=128):
            a, b = CI[name]
            return ci[p0:p1, a:b]

        def f(name, p0=0, p1=128):
            a, b = FS[name]
            return fs[p0:p1, a:b]

        ident = c("ident")

        x3T = sb("x3T", [128, 4, 2048])
        qT = sb("qT", [128, RQ, 2, 512])
        tail = sb("tail", [128, 8, 512])
        RA = sb("RA", [128, 5 * 2048])
        wq = sb("wq", [128, 4, 1024])
        wo = wq[:, :, 512:1024]
        d1 = RA[:, 0:2048].rearrange("p (k n) -> p k n", k=4)
        d2 = RA[:, 2048:4096].rearrange("p (k n) -> p k n", k=4)
        xs = RA[:, 4096:6144].rearrange("p (k n) -> p k n", k=4)
        x1T = RA[:, 6144:8192].rearrange("p (k n) -> p k n", k=4)
        x2T = RA[:, 8192:10240].rearrange("p (k n) -> p k n", k=4)
        wt = x3T[:, :, 1024:1536]
        wp = x3T[:, :, 1536:2048]
        at = sb("at", [128, 4, 64])
        bt = sb("bt", [128, 4, 64])
        v1 = sb("v1", [64, 512])
        v2 = sb("v2", [128, 512])
        z1 = sb("z1", [64, 512])
        z2 = sb("z2", [128, 512])
        stage = tail[:, 0:2, :].rearrange("p a (b n) -> p (a b) n", n=64)
        mk1 = sb("mk1", [64, 32])
        mk2 = sb("mk2", [128, 32])
        w0i = sb("w0i", [128, 16], I32)
        qr = sb("qr", [128, 2, 512])
        tab = {(n, h): sb(f"tab{n}{h}", [128, 16, 2, 32]) for n in "qk" for h in "ab"}
        sq = sb("sq", [128, 512])
        yy = sb("yy", [128, 512])
        t1 = sb("t1", [128, 512])
        t2 = sb("t2", [128, 512])
        ss = sb("ss", [128, 2, 8])
        gg = sb("gg", [128, 4, 2, 32])
        nt = sb("nt", [128, 2, 512])
        KVo = sb("KVo", [128, RO, 4, 512])
        lastKV = KVo[:, RO - 1, :, :].rearrange("p a n -> p (a n)")
        w0 = lastKV[:, 0:1024].rearrange("p (a b n) -> p a b n", a=2, b=4)
        u1 = lastKV[:, 1024:1280].rearrange("p (k n) -> p k n", k=4)
        u2 = lastKV[:, 1280:1792].rearrange("p (k n) -> p k n", k=4)
        thr = sb("thr", [128, 32])
        nmx = sb("nmx", [128, 128])
        sm = sb("sm", [128, 128])
        rs = sb("rs", [128, 128])
        io = sb("io", [128, 2, 32], U32)
        iw = sb("iw", [128, 2, 32], U32)
        inw = sb("inw", [128, 16], U32)

        at_ = [0]

        def ra(n, pattern, **k):
            at_[0] += n
            return RA[:, at_[0] - n:at_[0]].rearrange(pattern, **k)

        ks = ra(1280, "p (r g n) -> p r g n", r=2, g=2)
        Sp = ra(320 * RS, "p (r n) -> p r n", r=RS)
        Pp = ra(384 * RP, "p (r n) -> p r n", r=RP)
        PT = ra(384 * RT, "p (r n) -> p r n", r=RT)
        Os = ra(512, "p (r n) -> p r n", r=2)
        oT = ra(1024, "p (r g h n) -> p r g h n", r=2, g=2, h=2)
        Fo = ra(1024, "p (r n) -> p r n", r=2)
        mask = ra(640, "p (r n) -> p r n", r=2)
        KVn = ra(2048, "p (r n) -> p r n", r=4)

        tmp = tail[:, 2:8, :].rearrange("p a n -> p (a n)")
        E = tmp[0:32, 0:672].rearrange("p (i b) -> p i b", b=32)
        MA = tmp[:, 672:1344]
        MB = tmp[0:32, 1344:2016]
        CA = tmp[:, 2016:2176]
        CB = tmp[0:32, 2176:2336]
        r336 = tmp[0:32, 2336:2672]
        w336 = tmp[0:32, 2672:3008]
        idx = x3T[:, 1, 512:1024]
        rows = idx[0:32, 0:256]
        win = tail[0:32, 1, 0:320]
        wine = tail[0:32, 0, 0:320]
        small = sb("small", [128, 160])
        ti = sb("ti", [128, 24], I32)
        blk = sb("blk", [32, 21], I32)
        kvf = small[:, 0:1]
        rf = small[:, 1:2]
        oh = small[0:32, 2:18]
        blkf = small[0:32, 18:39]
        bwA = small[:, 39:40]
        bwB = small[0:32, 40:41]
        tA = small[:, 41:57]
        vA = small[:, 57:73]
        gA = small[:, 73:89]
        tB = small[0:32, 89:105]
        vB = small[0:32, 105:121]
        gB = small[0:32, 121:137]
        VA = small[:, 137:153]
        ones = sb("ones", [32, 128])
        VB = sb("VB", [32, 16])

        ringA = Ring(psum)
        ringS = Ring(psum[0:3])
        ringT = Ring(psum[3:6])
        ringO = Ring([psum[6]])
        ringF = Ring([psum[7]])

        block = ctx.enter_context(nc.Block())

        PAIRS = range(NPAIR)
        HEADS = [(b, g) for b in range(NB) for g in range(4)]

        @block.tensor
        def _(pe):
            def need(*key):
                book.need(pe, "pe", *key)

            def done(ins, *key):
                book.done(ins, "pe", *key)

            mm, tr = nc.tensor.matmul, nc.tensor.transpose

            def layer0(G):
                need("ld", "x", G)
                need("w0", G)
                if G >= 1:
                    need("x2", G - 1, 3)
                for fc in range(4):
                    ps = ringA.take(need, ("x1", G, fc), [("x1c", G, fc)])
                    for p in range(4):
                        ins = mm(ps[:, p * 128:(p + 1) * 128], xs[:, p, fc * 128:(fc + 1) * 128], w0[:, G % 2, p, :],
                                 start=True, stop=True)
                    done(ins, "x1", G, fc)

            def factors():
                need("ld", "wt")
                need("ld", "at")
                ps = ringA.take(need, ("u1",), [("u1c",)])
                for i in range(4):
                    for j in range(4):
                        ins = mm(ps[:, i * 64:(i + 1) * 64], wt[:, j, i * 128:(i + 1) * 128], at[:, j, :],
                                 start=(j == 0), stop=(j == 3))
                done(ins, "u1")
                need("ld", "wp")
                need("ld", "bt")
                ps = ringA.take(need, ("v1",), [("v1c",)])
                for j in range(4):
                    ins = mm(ps[0:64, :], bt[:, j, :], wp[:, j, :], start=(j == 0), stop=(j == 3))
                done(ins, "v1")

            def low(G, s, src, dense, u, z, v, M):
                pre = ("x1c", "x2c")[s - 1]
                ps = ringA.take(need, (f"z{s}", G), [(f"z{s}c", G)])
                for k in range(4):
                    need(pre, G, k)
                    ins = mm(ps[0:M, :], u[:, k, :], src[:, k, :], start=(k == 0), stop=(k == 3))
                done(ins, f"z{s}", G)
                for o in range(4):
                    ps = ringA.take(need, (f"x{s + 1}", G, o), [(f"x{s + 1}c", G, o)])
                    for k in range(4):
                        mm(ps[:, :], dense[:, k, o * 128:(o + 1) * 128], src[:, k, :], start=(k == 0), stop=False)
                    need(f"z{s}c", G)
                    ins = mm(ps[:, :], v[0:M, o * 128:(o + 1) * 128], z[0:M, :], start=False, stop=True)
                    done(ins, f"x{s + 1}", G, o)

            def kv(p):
                G = p // 4
                ps = ringA.take(need, ("kv", p), [("kvv", p), ("ksq", p), ("ky", p)])
                for k in range(4):
                    need("x3c", G, k)
                    ins = mm(ps[:, :], x3T[:, k, p * 128:(p + 1) * 128], wq[:, k, 512:1024], start=(k == 0), stop=(k == 3))
                done(ins, "kv", p)

            def q(p):
                ps = ringF.take(need, ("q", p), [("qsq", p), ("qy", p)])
                for k in range(4):
                    ins = mm(ps[:, :], x3T[:, k, p * 128:(p + 1) * 128], wq[:, k, 0:512], start=(k == 0), stop=(k == 3))
                done(ins, "q", p)

            def qt(p):
                need("qr", p)
                ps = ringT.take(need, ("qt", p), [("qtc", p)])
                for gp in range(2):
                    for h in range(2):
                        o = ps[:, gp * 256:(gp + 1) * 256].rearrange("p (b h t) -> p h b t", b=2, h=2)[:, h]
                        ins = tr(o, qr[:, p % 2, h * 256 + gp * 128:h * 256 + gp * 128 + 128], ident)
                done(ins, "qt", p)

            def index_old():
                need("rows")
                ps = ringA.take(need, ("io",), [("ioc",)])
                for j in range(2):
                    ins = tr(ps[:, j * 32:(j + 1) * 32], rows[:, j * 128:(j + 1) * 128], c("ident", 0, 32)[:, 0:32])
                done(ins, "io")

            def index_spread():
                need("E")
                ps0 = ringA.take(need, ("spA",), [("MA0",), ("MB0",)])
                mm(ps0[:, 0:320], ones[:, :], E[:, 0:10, :], start=True, stop=True)
                ps1 = ringA.take(need, ("spB",), [("MA1",), ("MB1",), ("CA",), ("CB",)])
                mm(ps1[:, 0:352], ones[:, :], E[:, 10:21, :], start=True, stop=True)
                ps = ringA.take(need, ("bw",), [("bwc",), ("bwd",)])
                mm(ps[:, 0:1], E[:, 16:20, :], ones[:, 0:1], start=True, stop=True)
                ins = mm(ps[0:32, 8:9], E[:, 20, :], ones[:, 0:1], start=True, stop=True)
                done(ins, "bw")

            def index_kill():
                need("CA")
                need("CB")
                need("vA")
                need("vB")
                ps = ringA.take(need, ("kill",), [("VA",), ("VB",)])
                mm(ps[:, 0:16], CA[:, 0:128], vA, start=True, stop=False)
                mm(ps[:, 0:16], CB[:, 0:128], vB, start=False, stop=True)
                mm(ps[0:32, 16:32], CA[:, 128:160], vA, start=True, stop=False)
                ins = mm(ps[0:32, 16:32], CB[:, 128:160], vB, start=False, stop=True)
                done(ins, "kill")

            def index_win():
                for k in ("VA", "VB", "MA0", "MB0", "MA1", "MB1"):
                    need(k)
                ps = ringA.take(need, ("win",), [("w336",)])
                for i in range(21):
                    mm(ps[0:32, i * 16:(i + 1) * 16], MA[:, i * 32:(i + 1) * 32], VA, start=True, stop=False)
                    ins = mm(ps[0:32, i * 16:(i + 1) * 16], MB[:, i * 32:(i + 1) * 32], VB[:, :], start=False, stop=True)
                done(ins, "win")

            def index_winT():
                need("wine")
                i32 = c("ident", 0, 32)[:, 0:32]
                ps = ringA.take(need, ("wt",), [("iwc",), ("inwc",), ("inwd",)])
                for j in range(2):
                    tr(ps[:, j * 32:(j + 1) * 32], wine[:, j * 128:(j + 1) * 128], i32)
                ins = tr(ps[0:64, 64:96], wine[:, 256:320], i32)
                done(ins, "wt")

            need("ld", "cf")
            layer0(0)
            factors()
            need("u1c")
            need("d1")
            need("ld", "u2")
            for G in range(NG):
                if G == 0:
                    need("v1c")
                low(G, 1, x1T, d1, u1, z1, v1, 64)
                if G == 0:
                    index_old()
                if G < NG - 1:
                    layer0(G + 1)
                if G == 0:
                    need("d2")
                    need("ld", "v2")
                    index_spread()
                if G == 1:
                    index_winT()
                low(G, 2, x2T, d2, u2, z2, v2, 128)
                if G == 0:
                    need("ld", "wq")
                for p in range(4 * G, 4 * G + 4):
                    kv(p)
                if G == 0:
                    index_kill()
                if G == 0:
                    index_win()
            def keys(b):
                p, h = b // 2, b % 2
                for c_ in range(2):
                    need("old", b, c_)
                    need("patch", b, c_)
                need("new", p)
                for gp in range(2):
                    ps = ringT.take(need, ("kt", b, gp), [("ktc", b, gp)])
                    for c_ in range(2):
                        tr(ps[:, c_ * 128:(c_ + 1) * 128], KVo[:, p % RO, h * 2 + c_, gp * 128:(gp + 1) * 128], ident)
                    hs = slice(h * 64, h * 64 + 64)
                    ins = tr(ps[:, 256:320], KVn[hs, p % 4, gp * 128:(gp + 1) * 128], c("ident", h * 64, h * 64 + 64)[:, hs])
                    done(ins, "kt", b, gp)

            def scores(n):
                b, g = HEADS[n]
                p, h, gp, g2 = b // 2, b % 2, g // 2, g % 2
                need("qtc", p)
                need("ktc", b, gp)
                ps = ringS.take(need, ("s", n), [("sp", n)])
                ins = mm(ps[:, 0:320], qT[:, p % RQ, g2, gp * 256 + h * 128:gp * 256 + h * 128 + 128], ks[:, b % 2, gp, :],
                         start=True, stop=True)
                done(ins, "s", n)

            def turn(n):
                b, g = HEADS[n]
                need("exp", n)
                ps = ringT.take(need, ("pt", n), [("ptc", n)])
                for c_ in range(2):
                    tr(ps[:, c_ * 128:(c_ + 1) * 128], Pp[:, n % RP, c_ * 128:(c_ + 1) * 128], ident)
                a = 256 - 64 * (b % 2)
                ins = tr(ps[:, 256:384], Pp[:, n % RP, a:a + 128], ident)
                done(ins, "pt", n)

            def values(n):
                b, g = HEADS[n]
                p, h = b // 2, b % 2
                if g == 0:
                    ringO.take(need, ("o", b), [("oc", b)])
                ps = ringO.where[("o", b)]
                need("ptc", n)
                o = ps[:, g * 64:(g + 1) * 64]
                for c_ in range(2):
                    mm(o, PT[:, n % RT, c_ * 128:(c_ + 1) * 128], KVo[:, p % RO, h * 2 + c_, 256 + g * 64:320 + g * 64],
                       start=(c_ == 0), stop=False)
                hs = slice(h * 64, h * 64 + 64)
                ins = mm(o, PT[hs, n % RT, 256:384], KVn[hs, p % 4, 256 + g * 64:320 + g * 64], start=False, stop=True)
                done(ins, "pv", n)

            def turn_out(b):
                need("oc", b)
                ps = ringT.take(need, ("ot", b), [("otc", b)])
                for gp in range(2):
                    ins = tr(ps[:, gp * 128:(gp + 1) * 128], Os[:, b % 2, gp * 128:(gp + 1) * 128], ident)
                done(ins, "ot", b)

            def final(p):
                need("ld", "wo")
                ps = ringF.take(need, ("f", p), [("fc", p)])
                for k in range(4):
                    mm(ps[:, k * 128:(k + 1) * 128], x3T[:, k, p * 128:(p + 1) * 128], ident, is_transpose=True,
                       start=(k == 0), stop=False, skip_group_check=True)
                need("otc", 2 * p)
                need("otc", 2 * p + 1)
                for k in range(4):
                    ins = mm(ps[:, :], oT[:, p % 2, k // 2, k % 2, :], wo[:, k, :], start=False, stop=(k == 3),
                             skip_group_check=True)
                done(ins, "f", p)

            for r in (*ringA.readers,):
                for k in r:
                    need(*k)
            q(0)
            q(1)
            qt(0)
            q(2)
            qt(1)
            keys(0)
            for n in range(128 + LF + 2):
                if n % 8 == 2 and n >= 8 and n // 8 + 2 < NPAIR:
                    q(n // 8 + 2)
                if n % 8 == 0 and 2 <= n // 8 + 1 < NPAIR:
                    qt(n // 8 + 1)
                if n % 4 == 1 and n // 4 + 1 < NB:
                    keys(n // 4 + 1)
                if n < 128:
                    scores(n)
                if 0 <= n - LT < 128:
                    turn(n - LT)
                if 0 <= n - LV < 128:
                    values(n - LV)
                if n >= LO and (n - LO) % 4 == 0 and (n - LO) // 4 < NB:
                    turn_out((n - LO) // 4)
                if n - 4 >= LF and (n - 4 - LF) % 8 == 0 and (n - 4 - LF) // 8 < NPAIR:
                    final((n - 4 - LF) // 8)

        @block.scalar
        def _(act):
            def need(*key):
                book.need(act, "act", *key)

            def done(ins, *key):
                book.done(ins, "act", *key)

            need("ang")
            for n in range(2):
                ins = nc.scalar.activation((t1, t2)[n][:, :], (sq, yy)[n][:, :], ACT.Sin)
            done(ins, "sincos")

            def x1c(G):
                if G >= 1:
                    need("x2", G - 1, 3)
                for fc in range(4):
                    need("x1", G, fc)
                    done(nc.scalar.copy(x1T[:, fc, :], ringA.where[("x1", G, fc)][:, :]), "x1c", G, fc)

            x1c(0)
            need("u1")
            done(nc.scalar.copy(u1[:, :, :].rearrange("p a b -> p (a b)"), ringA.where[("u1",)][:, 0:256]), "u1c")
            for G in range(NG):
                for o in (0, 2):
                    if G >= 1:
                        need("x3", G - 1, 3)
                    need("x2", G, o)
                    done(nc.scalar.copy(x2T[:, o, :], ringA.where[("x2", G, o)][:, :]), "x2c", G, o)
                if G < NG - 1:
                    x1c(G + 1)
                for o in (0, 2):
                    need("x3", G, o)
                    done(nc.scalar.copy(x3T[:, o, G * 512:(G + 1) * 512], ringA.where[("x3", G, o)][:, :]), "x3c", G, o)

                need("tab")
                for p in range(4 * G, 4 * G + 4):
                    need("kv", p)
                    if p >= 2:
                        need("ld", "n", p - 2)
                    done(nc.scalar.copy(nt[:, p % 2, 256:512], ringA.where[("kv", p)][:, 256:512]), "kvv", p)
                    if p >= 1:
                        need("kss", p - 1)
                    done(nc.scalar.square(sq[:, 0:256], ringA.where[("kv", p)][:, 0:256]), "ksq", p)
                    need("ks1", p)
                    done(nc.scalar.sqrt(ss[:, 0, 0:4], ss[:, 0, 0:4]), "kroot", p)

            def qsquare(p):
                need("q", p)
                need("kss", 15)
                if p >= 1:
                    need("qss", p - 1)
                done(nc.scalar.square(sq[:, :], ringF.where[("q", p)][:, :]), "qsq", p)

            def qroot(p):
                need("qs1", p)
                done(nc.scalar.sqrt(ss[:, 1, :], ss[:, 1, :]), "qroot", p)

            def qtc(p):
                need("qt", p)
                need("qzero")
                if p >= RQ:
                    need("s", 8 * (p - RQ) + 7)
                for g2 in range(2):
                    a = slice(g2 * 64, g2 * 64 + 64)
                    ins = nc.scalar.copy(qT[a, p % RQ, g2, :], ringT.where[("qt", p)][a, :])
                done(ins, "qtc", p)

            for p in range(3):
                qsquare(p)
                qroot(p)
                if p >= 1:
                    qtc(p - 1)

            def ktc(b):
                need("x3", 3, 3)
                need("kt", b, 0)
                if b >= 2:
                    need("s", 4 * (b - 2) + 1)
                done(nc.scalar.copy(ks[:, b % 2, 0, :], ringT.where[("kt", b, 0)][:, 0:320]), "ktc", b, 0)

            ktc(0)
            for n in range(128 + LF + 6):
                if n % 8 == 2 and n >= 8 and n // 8 + 2 < NPAIR:
                    qsquare(n // 8 + 2)
                if n % 8 == 0 and 2 <= n // 8 + 1 < NPAIR:
                    qtc(n // 8 + 1)
                if n % 4 == 1 and n // 4 + 1 < NB:
                    ktc(n // 4 + 1)
                if n % 8 == 3 and n >= 8 and n // 8 + 2 < NPAIR:
                    qroot(n // 8 + 2)
                if n < 128:
                    need("sp", n)
                    need("pzero")
                    if n >= RP:
                        need("pt", n - RP)
                    done(nc.scalar.activation(Pp[:, n % RP, 0:320], Sp[:, n % RS, :], ACT.Exp, bias=nmx[:, n:n + 1],
                                              scale=-1.0, accum_out=sm[:, n:n + 1]), "exp", n)
                m = n - LT
                if 0 <= m < 128 and m % 2 == 0:
                    need("pt", m)
                    if m >= RT:
                        need("pv", m - RT)
                    done(nc.scalar.copy(PT[:, m % RT, :], ringT.where[("pt", m)][:, 0:384]), "ptc", m)
                if n - 5 >= LF and (n - 5 - LF) % 8 == 0 and (n - 5 - LF) // 8 < NPAIR:
                    p = (n - 5 - LF) // 8
                    need("f", p)
                    if p >= 2:
                        need("ld", "out", p - 2)
                    done(nc.scalar.copy(Fo[:, p % 2, :], ringF.where[("f", p)][:, :]), "fc", p)

        @block.vector
        def _(dve):
            def need(*key):
                book.need(dve, "dve", *key)

            def done(ins, *key):
                book.done(ins, "dve", *key)
                return key

            v = nc.vector

            def step(ins, *key):
                done(ins, *key)
                need(*key)

            need("ld", "ci")
            done(v.tensor_scalar(w0i[:, :], cint("cond"), 64, None, ALU.mult), "w0i0")
            step(v.tensor_scalar(ti[:, 0:1], cint("kvw"), 4, None, ALU.arith_shift_right), "ti0")
            done(v.tensor_scalar(ti[:, 1:2], cint("kvw"), 15, None, ALU.bitwise_and), "ti1")
            done(v.tensor_tensor(w0i[:, :], w0i[:, :], cint("c").to_broadcast([128, 16]), ALU.add), "w0i")
            done(v.tensor_tensor(ti[:, 2:3], ti[:, 0:1], cint("b257"), ALU.add), "ti")
            done(v.memset(w0[:, :, :, :], 0.0), "w0z")
            done(v.memset(ones[:, :], 1.0), "ones")
            done(v.memset(qT[:, :, :, :], 0.0), "qzero")
            need("ti1")
            need("ld", "cf")
            need("ld", "fs")
            step(v.tensor_copy(rf, ti[:, 1:2]), "rf")
            step(v.tensor_scalar(oh, c("iota16", 0, 32), rf[0:32, :], None, ALU.is_equal), "oh")
            done(v.tensor_scalar(mk1[:, :], cint("idx1", 0, 64), c("e", 0, 64), None, ALU.is_equal), "mk1")
            done(v.tensor_scalar(mk2[:, :], cint("idx2"), c("e"), None, ALU.is_equal), "mk2")
            done(v.tensor_scalar(thr[:, :], cint("kvall"), -256.0, BIGC, ALU.add, ALU.mult), "thr")
            need("w0z")

            def blockdiag(G):
                need("ld", "stage", G)
                if G >= 2:
                    need("x1", G - 2, 3)
                for h in range(2):
                    a = slice(h * 64, h * 64 + 64)
                    idb = c("ident", h * 64, h * 64 + 64)[:, a]
                    ins = v.tensor_tensor(w0[a, G % 2, :, a], stage[a, 4 * G:4 * G + 4, :],
                                          idb.unsqueeze(1).to_broadcast([64, 4, 64]), ALU.add)
                done(ins, "w0", G)

            blockdiag(0)
            ang = t1[:, :].rearrange("p (a d) -> p a d", a=16)
            kvt = small[:, 2:18]
            kvg = t2[:, 0:16]
            step(v.tensor_copy(kvg, cint("kvtok")), "kvg0")
            step(v.tensor_scalar(kvg, kvg, c("t"), None, ALU.add), "kvg")
            step(v.tensor_tensor(ang, kvg.unsqueeze(2).to_broadcast([128, 16, 32]),
                                 c("inv").unsqueeze(1).to_broadcast([128, 16, 32]), ALU.mult), "ang0")
            A = t1[:, :]
            n_, m_ = idx[:, :], t2[:, :]
            for i, (dst, off) in enumerate(((sq[:, :], 0.0), (yy[:, :], 0.25))):
                step(v.tensor_scalar(n_, A, float(1.0 / TWO_PI), off, ALU.mult, ALU.add), "rr", i, 0)
                step(v.tensor_scalar(m_, n_, MAGIC, None, ALU.add), "rr", i, 1)
                step(v.tensor_scalar(n_, m_, -MAGIC, None, ALU.add), "rr", i, 2)
                step(v.scalar_tensor_tensor(dst, n_, -C1, A, ALU.mult, ALU.add), "rr", i, 3)
                step(v.scalar_tensor_tensor(m_, n_, -C2, dst, ALU.mult, ALU.add), "rr", i, 4)
                step(v.scalar_tensor_tensor(dst, n_, -C3, m_, ALU.mult, ALU.add), "rr", i, 5)
                if off:
                    step(v.tensor_scalar(dst, dst, float(np.pi / 2), None, ALU.add), "rr", i, 6)
                step(v.tensor_scalar(dst, dst, 3.1415925, -3.1415925, ALU.min, ALU.max), "rr", i, 7)
            done(v.tensor_copy(gg[:, 0, 0, 0:1], dst[:, 0:1]), "ang")
            need("ang")
            for n, nm in enumerate(("qs", "ks")):
                s2 = f(nm).rearrange("p (a b) -> p a b", a=2)
                v.tensor_scalar(gg[:, 2 * n, :, :], s2, 1.0, 8.0, ALU.add, ALU.mult)
                v.tensor_scalar(gg[:, 2 * n + 1, 0, :], s2[:, 1, :], 1.0, -8.0, ALU.add, ALU.mult)
                ins = v.tensor_scalar(gg[:, 2 * n + 1, 1, :], s2[:, 0, :], 1.0, 8.0, ALU.add, ALU.mult)
            done(ins, "gg")
            need("ld", "blk")
            step(v.tensor_copy(blkf, blk[:, :]), "blkf")
            step(v.scalar_tensor_tensor(r336.rearrange("p (i o) -> p i o", o=16),
                                        blkf.unsqueeze(2).to_broadcast([32, 21, 16]), 16.0,
                                        c("iota16", 0, 32).unsqueeze(1).to_broadcast([32, 21, 16]), ALU.mult, ALU.add), "r336")
            done(v.tensor_tensor(E, blkf.unsqueeze(2).to_broadcast([32, 21, 32]),
                                 c("ident", 0, 32)[:, 0:32].unsqueeze(1).to_broadcast([32, 21, 32]), ALU.mult), "E")
            step(v.tensor_scalar(rows, r336[:, 0:256], oh[:, 0:1], None, ALU.mult), "rows", 0)
            for k in range(1, 16):
                step(v.scalar_tensor_tensor(rows, r336[:, k:k + 256], oh[:, k:k + 1], rows, ALU.mult, ALU.add), "rows", k)
            done(v.tensor_copy(kvf, rf), "rows")
            need("v1")
            done(v.tensor_scalar(v1[:, :], ringA.where[("v1",)][0:64, :], f("s1", 0, 64), None, ALU.mult), "v1c")
            need("ld", "d1")
            for k in range(4):
                o = d1[:, k, k * 128:(k + 1) * 128]
                ins = v.tensor_tensor(o, o, ident, ALU.add)
            done(ins, "d1")
            for nm, P, t_, v_, g_, m16, val in (("A", 128, tA, vA, gA, "m16", "val"), ("B", 32, tB, vB, gB, "m16b", "valb")):
                step(v.tensor_scalar(t_, c("iota16", 0, P), c(m16, 0, P), rf[0:P, :], ALU.add, ALU.subtract), "t", nm)
                v.tensor_scalar(v_, t_, 0.0, None, ALU.is_ge)
                step(v.tensor_scalar(g_, t_, 63.0, None, ALU.is_le), "le", nm)
                step(v.tensor_tensor(v_, v_, g_, ALU.mult), "v" + nm)
                step(v.tensor_scalar(g_, t_, c(val, 0, P), None, ALU.add), "g", nm)

            need("sincos")
            need("gg")
            sin = t1[:, :].rearrange("p (a d) -> p a d", a=16).unsqueeze(2).to_broadcast([128, 16, 2, 32])
            cos = t2[:, :].rearrange("p (a d) -> p a d", a=16).unsqueeze(2).to_broadcast([128, 16, 2, 32])
            for n, nm in enumerate("qk"):
                v.tensor_tensor(tab[nm, "a"][:, :, :, :], cos, gg[:, 2 * n, :, :].unsqueeze(1).to_broadcast([128, 16, 2, 32]),
                                ALU.mult)
                ins = v.tensor_tensor(tab[nm, "b"][:, :, :, :], sin,
                                      gg[:, 2 * n + 1, :, :].unsqueeze(1).to_broadcast([128, 16, 2, 32]), ALU.mult)
            done(ins, "tab")
            need("tab")

            def match():
                need("bw")
                v.tensor_copy(bwA, ringA.where[("bw",)][:, 0:1])
                done(v.tensor_copy(bwB, ringA.where[("bw",)][0:32, 8:9]), "bwc")
                need("bwc")
                book.new[("bwd",)] = book.new[("bwc",)]
                a, b_ = ringA.where[("spA",)], ringA.where[("spB",)]
                done(v.tensor_scalar(MA[:, 0:320], a[:, 0:320], bwA, None, ALU.is_equal), "MA0")
                done(v.tensor_scalar(MA[:, 320:672], b_[:, 0:352], bwA, None, ALU.is_equal), "MA1")
                done(v.tensor_scalar(MB[:, 0:320], a[0:32, 0:320], bwB, None, ALU.is_equal), "MB0")
                done(v.tensor_scalar(MB[:, 320:672], b_[0:32, 0:352], bwB, None, ALU.is_equal), "MB1")
                done(v.scalar_tensor_tensor(CA, b_[:, 192:352], bwA, c("la"), ALU.is_equal, ALU.mult), "CA")
                done(v.scalar_tensor_tensor(CB, b_[0:32, 192:352], bwB, c("lb", 0, 32), ALU.is_equal, ALU.mult), "CB")

            def survive():
                need("kill")
                ps = ringA.where[("kill",)]
                for nm, P, o, t_, v_, g_, V in (("A", 128, 0, tA, vA, gA, VA), ("B", 32, 16, tB, vB, gB, VB[:, :])):
                    step(v.tensor_scalar(t_, ps[0:P, o:o + 16], 0.0, None, ALU.is_equal), "alive", nm)
                    step(v.tensor_tensor(t_, t_, v_, ALU.mult), "alive2", nm)
                    done(v.tensor_tensor(V, t_, g_, ALU.mult), "V" + nm)

            def winners():
                need("win")
                step(v.tensor_copy(w336, ringA.where[("win",)][0:32, 0:336]), "w336")
                step(v.tensor_scalar(win, w336[:, 0:320], oh[:, 0:1], None, ALU.mult), "winner", 0)
                for k in range(1, 16):
                    w = min(320, 336 - k)
                    step(v.scalar_tensor_tensor(win[:, 0:w], w336[:, k:k + w], oh[:, k:k + 1], win[:, 0:w], ALU.mult,
                                                ALU.add), "winner", k)
                step(v.tensor_scalar(wine, win, 0.0, SKIP, ALU.is_equal, ALU.mult), "wine0")
                step(v.scalar_tensor_tensor(wine, win, -1.0, wine, ALU.add, ALU.add), "wine")

            def indices():
                need("wt")
                ps = ringA.where[("wt",)]
                done(v.tensor_copy(iw[:, :, :].rearrange("p a b -> p (a b)"), ps[:, 0:64]), "iwc")
                pr = ps[0:64, 64:96].rearrange("p (a b) -> p b a", b=2)
                done(v.tensor_copy(inw[0:64, :], pr[:, 0, :]), "inwc")
                done(v.tensor_copy(inw[64:128, :], pr[:, 1, :]), "inwd")

            def zc(G, s, z, mk, M):
                need(f"z{s}", G)
                need("mk1")
                need("mk2")
                if G >= 1:
                    need(f"x{s + 1}", G - 1, 3)
                done(v.tensor_tensor(z[0:M, :].rearrange("p (b t) -> p b t", b=8),
                                     ringA.where[(f"z{s}", G)][0:M, :].rearrange("p (b t) -> p b t", b=8),
                                     mk[0:M, 8 * G:8 * G + 8].unsqueeze(2).to_broadcast([M, 8, 64]), ALU.mult), f"z{s}c", G)

            def rope(kind, p, nh, dst, parts=(0, 1, 2, 3)):
                w = nh * 64
                k0 = kind[0]
                r = ss[:, 0 if k0 == "k" else 1, 0:nh]
                y = yy[:, 0:w].rearrange("p (h a d) -> p h a d", a=2, d=32)
                a, b_ = tab[k0, "a"][:, p, :, :], tab[k0, "b"][:, p, :, :]
                if 0 in parts:
                    need(k0 + "sq", p)
                    step(v.tensor_reduce(r, sq[:, 0:w].rearrange("p (h d) -> p h d", d=64), AX.X, ALU.add), k0 + "ss", p)
                    done(v.tensor_scalar(r, r, 64e-6, None, ALU.add), k0 + "s1", p)
                if 1 in parts:
                    need(k0 + "root", p)
                    step(v.reciprocal(r, r), k0 + "s2", p)
                    done(v.tensor_tensor(yy[:, 0:w].rearrange("p (h d) -> p h d", d=64),
                                         (ringA if k0 == "k" else ringF).where[(kind, p)][:, 0:w].rearrange(
                                             "p (h d) -> p h d", d=64),
                                         r.unsqueeze(2).to_broadcast([128, nh, 64]), ALU.mult), k0 + "y", p)
                if 2 in parts:
                    need(k0 + "y", p)
                    v.tensor_tensor(t1[:, 0:w].rearrange("p (h a d) -> p h a d", a=2, d=32), y,
                                    a.unsqueeze(1).to_broadcast([128, nh, 2, 32]), ALU.mult)
                    t2v = t2[:, 0:w].rearrange("p (h a d) -> p h a d", a=2, d=32)
                    for a_ in range(2):
                        ins = v.tensor_tensor(t2v[:, :, a_, :], y[:, :, 1 - a_, :],
                                              b_[:, a_, :].unsqueeze(1).to_broadcast([128, nh, 32]), ALU.mult)
                    done(ins, k0 + "sum", p)
                if 3 in parts:
                    need(k0 + "sum", p)
                    if k0 == "q" and p >= 2:
                        need("qt", p - 2)
                    done(v.tensor_tensor(dst, t1[:, 0:w], t2[:, 0:w], ALU.add), {"k": "kr", "q": "qr"}[k0], p)

            def rope_q(p, *parts):
                rope("q", p, 8, qr[:, p % 2, :], parts)

            for G in range(NG):
                if G + 1 < NG:
                    blockdiag(G + 1) if G == 0 else None
                zc(G, 1, z1, mk1, 64)
                for o in (1, 3):
                    need("x2", G, o)
                    if G >= 1:
                        need("x3", G - 1, 3)
                    done(v.tensor_copy(x2T[:, o, :], ringA.where[("x2", G, o)][:, :]), "x2c", G, o)
                if G == 0:
                    need("io")
                    done(v.tensor_copy(io[:, :, :].rearrange("p a b -> p (a b)"), ringA.where[("io",)][:, 0:64]), "ioc")
                    need("ld", "d2")
                    for k in range(4):
                        o = d2[:, k, k * 128:(k + 1) * 128]
                        ins = v.tensor_tensor(o, o, ident, ALU.add)
                    done(ins, "d2")
                    need("ld", "v2")
                    done(v.tensor_scalar(v2[:, :], v2[:, :], f("s2"), None, ALU.mult), "v2")
                    match()
                    blockdiag(2)
                    blockdiag(3)
                    winners_after = True
                if G == 1:
                    indices()
                zc(G, 2, z2, mk2, 128)
                for o in (1, 3):
                    need("x3", G, o)
                    done(v.tensor_copy(x3T[:, o, G * 512:(G + 1) * 512], ringA.where[("x3", G, o)][:, :]), "x3c", G, o)
                for p in range(4 * G, 4 * G + 4):
                    if p >= 2:
                        need("ld", "n", p - 2)
                    rope("kv", p, 4, nt[:, p % 2, 0:256])
                if G == 0:
                    survive()
                if G == 0:
                    winners()

            need("x3", 3, 3)
            for r in range(3):
                ins = v.memset(Pp[:, r, 320:384], 0.0)
            done(ins, "pzero")
            for r in range(2):
                ins = v.tensor_copy(mask[:, r, 256:320], c("band")[:, 256:320])
            done(ins, "mask0")

            def maskb(b):
                done(v.scalar_tensor_tensor(mask[:, b % 2, 0:256], c("iotac"), thr[:, b:b + 1], c("band")[:, 0:256],
                                            ALU.add, ALU.min), "mask", b)

            def ktc(b):
                need("kt", b, 1)
                if b >= 2:
                    need("s", 4 * (b - 2) + 3)
                done(v.tensor_copy(ks[:, b % 2, 1, :], ringT.where[("kt", b, 1)][:, 0:320]), "ktc", b, 1)

            rope_q(0, 0, 1, 2, 3)
            rope_q(1, 0, 1, 2, 3)
            rope_q(2, 0, 1, 2, 3)
            maskb(0)
            ktc(0)
            for n in range(128 + LF + 2):
                if n % 4 == 1 and n // 4 + 1 < NB:
                    ktc(n // 4 + 1)
                    maskb(n // 4 + 1)
                if n >= 8 and n // 8 + 2 < NPAIR and n % 8 in (3, 4, 5, 6):
                    rope_q(n // 8 + 2, n % 8 - 3)
                if n < 128:
                    b = n // 4
                    need("s", n)
                    need("mask", b)
                    need("mask0")
                    if n >= RS:
                        need("exp", n - RS)
                    done(v.tensor_tensor_reduce(Sp[:, n % RS, :], ringS.where[("s", n)][:, 0:320], mask[:, b % 2, :],
                                                -0.0625, 3.0e38, ALU.add, ALU.min, nmx[:, n:n + 1]), "sp", n)
                m = n - LT
                if 0 <= m < 128 and m % 2 == 1:
                    need("pt", m)
                    if m >= RT:
                        need("pv", m - RT)
                    done(v.tensor_copy(PT[:, m % RT, :], ringT.where[("pt", m)][:, 0:384]), "ptc", m)
                m = n - LV
                if 0 <= m < 128 and m % 4 == 3:
                    b = m // 4
                    need("exp", m)
                    step(v.reciprocal(rs[:, 4 * b:4 * b + 4], sm[:, 4 * b:4 * b + 4]), "rs", b)
                    need("pv", m)
                    if b >= 2:
                        need("ot", b - 2)
                    done(v.tensor_tensor(Os[:, b % 2, :].rearrange("p (g d) -> p g d", g=4),
                                         ringO.where[("o", b)][:, 0:256].rearrange("p (g d) -> p g d", g=4),
                                         rs[:, 4 * b:4 * b + 4].unsqueeze(2).to_broadcast([128, 4, 64]), ALU.mult), "oc", b)
                if n >= LO and (n - LO) % 4 == 0 and (n - LO) // 4 < NB:
                    b = (n - LO) // 4
                    need("ot", b)
                    if b >= 4:
                        need("f", b // 2 - 2)
                    h = b % 2
                    for gp in range(2):
                        ins = v.tensor_copy(oT[:, (b // 2) % 2, gp, :, h * 64:h * 64 + 64],
                                            ringT.where[("ot", b)][:, gp * 128:(gp + 1) * 128].rearrange("p (h t) -> p h t", h=2))
                    done(ins, "otc", b)

        @block.gpsimd
        def _(pool):
            def need(*key):
                book.need(pool, "pool", *key)

            off = bass.IndirectOffsetOnAxis

            need("w0i")
            for G in range(4):
                for p in range(4 * G, 4 * G + 4):
                    ins = nc.gpsimd.indirect_dma_start(stage[:, p, :], None, W0[:, :],
                                                       off(ap=w0i[:, p:p + 1].bitcast(U32), axis=0))
                    book.done(ins, f"g_w{G}", "stage", p)
                book.new[("ld", "stage", G)] = book.new[("stage", 4 * G + 3)]
                if G == 0:
                    need("ti")
                    ins = nc.gpsimd.indirect_dma_start(blk[:, :], None, TBL[:, :],
                                                       off(ap=ti[0:32, 2:3].bitcast(U32), axis=0))
                    book.done(ins, "g_blk", "ld", "blk")

            def old(p):
                if p >= RO:
                    need("pv", 8 * (p - RO) + 7)
                for h in range(2):
                    for c_ in range(2):
                        b = 2 * p + h
                        ins = nc.gpsimd.indirect_dma_start(KVo[:, p % RO, h * 2 + c_, :], None, KV[:, :],
                                                           off(ap=io[:, c_, b:b + 1], axis=0))
                        book.done(ins, f"g_o{(p % RO)}_{h}{c_}", "old", b, c_)

            need("ioc")
            for p in range(RO):
                if p == RO - 1:
                    need("x1", 3, 3)
                    need("z2", 3)
                old(p)
            need("iwc")
            need("inwc")
            need("inwd")
            for p in PAIRS:
                need("ld", "n", p)
            for p in PAIRS:
                if p >= RO:
                    old(p)
                ins = nc.gpsimd.indirect_dma_start(KVn[:, p % 4, :], None, SCR[:, :], off(ap=inw[:, p:p + 1], axis=0))
                book.done(ins, f"g_n{p % 4}", "new", p)
                for h in range(2):
                    for c_ in range(2):
                        b = 2 * p + h
                        need("old", b, c_)
                        ins = nc.gpsimd.indirect_dma_start(KVo[:, p % RO, h * 2 + c_, :], None, SCR[:, :],
                                                           off(ap=iw[:, c_, b:b + 1], axis=0),
                                                           bounds_check=2047, oob_is_err=False)
                        book.done(ins, f"g_p{p % 4}_{h}{c_}", "patch", b, c_)

        @block.sync
        def _(sp):
            def need(*key):
                book.need(sp, "sp", *key)

            def load(dst, src, *key):
                book.done(nc.sync.dma_start(dst, src), "d_" + "_".join(map(str, key)), "ld", *key)

            load(ci[:, :], CID[:, :], "ci")
            load(cf[:, :], CFD[:, :], "cf")
            load(fs[:, :], FSD[:, :], "fs")
            need("ld", "stage", 0)
            load(xs, X[:, 0, :, :], "x", 0)
            load(wt, WT[:, :, :], "wt")
            load(at[:, :, :], AT[:, :, :], "at")
            load(wp, WP[:, :, :], "wp")
            load(bt[:, :, :], BT[:, :, :], "bt")
            load(d1, WB[:, :, :], "d1")
            load(u2[:, :, :], A2[:, :, :], "u2")
            load(v2[:, :], V2D[:, :], "v2")
            load(d2, W2[:, :, :], "d2")
            load(wq[:, :, :], WQKV[:, :, :], "wq")
            for G in range(NG):
                if G + 1 < NG:
                    need("x1", G, 3)
                    load(xs, X[:, G + 1, :, :], "x", G + 1)
                for p in range(4 * G, 4 * G + 4):
                    need("kr", p)
                    need("kvv", p)
                    load(SCR[p * 128:(p + 1) * 128, :], nt[:, p % 2, :], "n", p)
            need("kv", 15)
            load(wo, WO[:, :, :], "wo")
            for p in PAIRS:
                need("fc", p)
                load(out[p * 128:(p + 1) * 128, :], Fo[:, p % 2, :], "out", p)
            for p in PAIRS:
                need("ld", "out", p)


def _constants():
    cf = np.zeros((128, NCF), np.float32)
    ci = np.zeros((128, 2), np.int32)
    p = np.arange(128)

    def put(name, a):
        lo, hi = CF[name]
        cf[:a.shape[0], lo:hi] = a.reshape(a.shape[0], hi - lo)
    put("ident", np.eye(128, dtype=np.float32))
    t, s = (p % 64)[:, None], np.arange(320)[None, :]
    put("band", np.where((s > t) & (s <= t + 256), 0.0, -1e30))
    put("iotac", np.broadcast_to(np.arange(256) * BIGC, (128, 256)))
    m, b = np.divmod(np.arange(160), 32)
    order = b * 5 + m
    later = (order[:, None] > order[None, :]).astype(np.float32)
    put("la", later[:128])
    put("lb", later[128:])
    put("iota16", np.broadcast_to(np.arange(16.0), (128, 16)))
    half = np.float32(10000.0) ** (np.arange(32, dtype=np.float32) / np.float32(32))
    put("inv", np.broadcast_to((np.float32(1.0) / half).astype(np.float32), (128, 32)))
    put("t", (p % 64).astype(np.float32))
    put("e", (p // 16).astype(np.float32))
    put("m16", (p // 32 * 16.0))
    put("val", (p % 32 * 64.0 + 1))
    put("m16b", np.full(128, 64.0))
    put("valb", (p % 32 * 64.0 + 1))
    ci[:, 0] = p % 64
    ci[:, 1] = p * 257
    return cf, ci


def _layout(i):
    a = {k: np.asarray(v) for k, v in i.items()}
    cf, cc = _constants()
    cond, i1, i2, kv = (a[k].astype(np.int32) for k in ("itok_B_1_198", "itok_B_0_3", "itok_B_0_6", "itok_B_37_3939"))
    ci = np.zeros((128, NCI), np.int32)

    def put(name, v):
        lo, hi = CI[name]
        ci[:, lo:hi] = v

    def by_pair(v):
        return np.repeat(v.reshape(16, 2).T, 64, axis=0)
    put("cond", by_pair(cond))
    put("kvtok", by_pair(kv))
    put("idx1", i1[None, :])
    put("idx2", i2[None, :])
    put("kvall", kv[None, :])
    put("kvw", np.tile(kv, 4)[:, None])
    put("c", cc[:, 0:1])
    put("b257", cc[:, 1:2])
    fs = np.zeros((128, NFS), np.float32)
    fs[:, FS["qs"][0]:FS["qs"][1]] = a["L3_cond_q_norm_scale"][None, :]
    fs[:, FS["ks"][0]:FS["ks"][1]] = a["L3_cond_k_norm_scale"][None, :]
    fs[0:64, FS["s1"][0]] = np.repeat(a["L1_cond_scaling"], 16)
    fs[:, FS["s2"][0]] = np.repeat(a["L2_cond_scalings"], 16)

    def rows(w):
        return np.ascontiguousarray(w.reshape(4, 128, -1).transpose(1, 0, 2))
    tbl = a["itok_Bx257_0_4111"].astype(np.int32)
    at = np.clip(np.arange(257)[:, None] - 16 + np.arange(21)[None, :], 0, 256)
    tbl = np.ascontiguousarray(tbl[:, at].reshape(NB * 257, 21))
    Wq = a["L3_cond_Wq"].reshape(4, 2, 64, 512).transpose(1, 0, 2, 3).reshape(512, 512)
    wqkv = np.concatenate([Wq, a["L3_cond_Wk"], a["L3_cond_Wv"]], 0).T
    wo = a["L3_cond_Wo"].T.reshape(2, 2, 2, 64, 512).transpose(0, 2, 1, 3, 4).reshape(512, 512)
    kvr = np.empty((4112, 16, 2, 4, 64), np.float32)
    kvr[:, :, 0] = a["L3_cond_k_blocks"].transpose(0, 2, 1, 3)
    kvr[:, :, 1] = a["L3_cond_v_blocks"].transpose(0, 2, 1, 3)
    return {
        "X": np.ascontiguousarray(a["x"].reshape(4, 4, 128, 512).transpose(2, 0, 1, 3)),
        "W0": np.ascontiguousarray(a["L0_cond_weights"].reshape(12800, 64)),
        "WB": rows(a["L1_cond_W_base"].T),
        "WT": rows(a["L1_cond_Wt"]),
        "AT": rows(a["L1_cond_A"].reshape(64, 512).T),
        "BT": rows(a["L1_cond_B_w"].transpose(1, 0, 2).reshape(512, 64)),
        "WP": rows(a["L1_cond_Wp"].T),
        "W2": rows(a["L2_cond_W"].T),
        "A2": rows(a["L2_cond_A"].reshape(128, 512).T),
        "V2D": np.ascontiguousarray(a["L2_cond_Bm"].transpose(0, 2, 1).reshape(128, 512)),
        "WQKV": rows(wqkv),
        "WO": rows(wo),
        "KV": kvr.reshape(KVROWS, 512),
        "TBL": tbl,
        "CFD": cf,
        "CID": ci,
        "FSD": fs,
    }


def _build(make, arrays):
    known = None
    for _ in range(2):
        nc = make()
        args = {}
        for name, v in arrays.items():
            args[name] = nc.dram_tensor(f"in_{name}", v.shape, mybir.dt.from_np(v.dtype), kind="ExternalInput").ap()
        args["SCR"] = nc.dram_tensor("scratch", (2048, 512), F32, kind="Internal").ap()
        args["out"] = nc.dram_tensor("out_0_dram", (2048, 512), F32, kind="ExternalOutput").ap()
        book = Book(known)
        program(nc, book, **args)
        known = book.new
    return nc


def kernel(**inputs):
    import concourse.bacc as _bacc
    from concourse.bass_utils import run_bass_kernel_spmd as _run

    arrays = _layout(inputs)
    nc = _build(lambda: _bacc.Bacc("TRN2", target_bir_lowering=False, num_devices=1), arrays)
    r = _run(nc, [{f"in_{k}": v for k, v in arrays.items()}], core_ids=[0])
    return r.results[0]["out_0_dram"].reshape(NB, T, D)
```

```python
from contextlib import ExitStack

import numpy as np

import concourse.bass as bass
from concourse import mybir

F32 = mybir.dt.float32
F32R = mybir.dt.float32r
ARENA = 28160
I32 = mybir.dt.int32
U32 = mybir.dt.uint32
ALU = mybir.AluOpType
ACT = mybir.ActivationFunctionType
AX = mybir.AxisListType

NB, T, D, HD = 32, 64, 512, 64
NPAIR = 16
NG = 4
NBLK = 257
KVROWS = 4112 * 16
RO = 4
RQ = 3
RS, RP, RT = 3, 4, 3
LT, LV, LO, LF = 3, 5, 10, 15
NSTEP = 128 + LF
LATE = 2
SKIP = 65536.0
BIGC = float(2.0 ** 100)
MAGIC = 12582912.0
TWO_PI = 2.0 * np.pi
C1 = 6.28125
C2 = float(np.float32(np.round((TWO_PI - C1) * 2.0 ** 20) / 2.0 ** 20))
C3 = float(np.float32(TWO_PI - C1 - C2))

CF = {}
CI = {}


def _columns(table, widths):
    at = 0
    for name, w in widths:
        table[name] = (at, at + w)
        at += w
    return at


NCF = _columns(CF, [("ident", 128), ("band", 320), ("iotac", 256), ("la", 160), ("lb", 160), ("iota16", 16),
                    ("inv", 32), ("t", 1), ("e", 1), ("m16", 1), ("val", 1), ("m16b", 1), ("valb", 1)])
NCI = _columns(CI, [("cond", 16), ("kvtok", 16), ("idx1", 32), ("idx2", 32), ("kvall", 32), ("kvw", 1),
                    ("c", 1), ("b257", 1)])
FS = {}
NFS = _columns(FS, [("qs", 64), ("ks", 64), ("s1", 1), ("s2", 1)])


class Book:

    def __init__(self, known):
        self.known, self.new, self.count, self.seen, self.sem = known, {}, {}, {}, {}

    def start(self, nc, ctx):
        self.nc, self.ctx = nc, ctx

    def _sem(self, s):
        if s not in self.sem:
            self.sem[s] = self.ctx.enter_context(self.nc.semaphore("s_" + s))
        return self.sem[s]

    def done(self, ins, s, *key):
        n = 1 if s in ("pe", "act", "dve", "pool") else 16
        self.count[s] = self.count.get(s, 0) + n
        ins.then_inc(self._sem(s), n)
        assert key not in self.new, key
        self.new[key] = (s, self.count[s])

    def need(self, eng, who, *key):
        s, v = self.known.get(key, ("pe", 0)) if self.known is not None else ("pe", 0)
        if self.known and key not in self.known:
            raise KeyError(key)
        if self.seen.get((who, s), 0) < v:
            self.seen[(who, s)] = v
            eng.wait_ge(self._sem(s), v)


class Ring:

    def __init__(self, banks):
        self.banks, self.n, self.readers, self.where = banks, 0, [()] * len(banks), {}

    def take(self, need, key, readers):
        i = self.n % len(self.banks)
        self.n += 1
        for r in self.readers[i]:
            need(*r)
        self.readers[i] = readers
        self.where[key] = self.banks[i]
        return self.banks[i]


def program(nc, book, X, W0, WB, WT, AT, BT, WP, W2, A2, V2D, WQKV, WO, KV, TBL, CFD, CID, FSD, SCR, out):
    ctx = ExitStack()
    with ctx:
        book.start(nc, ctx)

        def sb(name, shape, dt=F32):
            return ctx.enter_context(nc.sbuf_tensor(name, shape, dt))

        psum = [ctx.enter_context(nc.psum_tensor(f"ps{i}", [128, 512], F32)) for i in range(8)]

        cf = sb("cf", [128, NCF])
        ci = sb("ci", [128, NCI], I32)
        fs = sb("fs", [128, NFS])

        def c(name, p0=0, p1=128):
            a, b = CF[name]
            return cf[p0:p1, a:b]

        def cint(name, p0=0, p1=128):
            a, b = CI[name]
            return ci[p0:p1, a:b]

        def f(name, p0=0, p1=128):
            a, b = FS[name]
            return fs[p0:p1, a:b]

        ident = c("ident")

        x3T = sb("x3T", [128, 4, 2048])
        sc = sb("sc", [128, 2, 512])
        tr_ = sb("tr_", [128, 2, 2, 32])
        KVo = sb("KVo", [128, RO, 4, 512])
        at = sb("at", [128, 4, 64])
        bt = sb("bt", [128, 4, 64])
        mk1 = sb("mk1", [64, 32])
        mk2 = sb("mk2", [128, 32])
        w0i = sb("w0i", [128, 16], I32)
        sq = sb("sq", [128, 512])
        yy = sb("yy", [128, 512])
        t1 = sb("t1", [128, 512])
        t2 = sb("t2", [128, 512])
        ss = sb("ss", [128, 3, 8])
        nw = sb("nw", [128, 2, 8])
        gg = sb("gg", [128, 4, 2, 32])
        nt = sb("nt", [128, 2, 512])
        thr = sb("thr", [128, 32])
        nmx = sb("nmx", [128, 128])
        sm = sb("sm", [128, 128])
        rs = sb("rs", [128, 128])
        io = sb("io", [128, 2, 32], U32)
        iw = sb("iw", [128, 2, 32], U32)
        inw = sb("inw", [128, 16], U32)

        base = nc.sbuf_base
        sb("arena", [128, ARENA])

        def place(name, at_, shape, dt=F32):
            n = int(np.prod(shape[1:]))
            assert at_ + n <= ARENA, name
            return nc.alloc_sbuf_tensor_at(name, shape, dt, offset=base + 4 * at_)

        def halves(name, at_, shape):
            n = int(np.prod(shape[1:]))
            return place(name + "h", at_, shape, F32R), place(name + "l", at_ + n, shape, F32R)

        d1 = halves("d1", 0, [128, 4, 512])
        d2 = halves("d2", 4096, [128, 4, 512])
        x2T = halves("x2T", 8192, [128, 4, 512])
        x13 = halves("x13", 12288, [128, 4, 512])
        wkv = halves("wkv", 16384, [128, 4, 512])
        u1 = halves("u1", 20480, [128, 4, 64])
        u2 = halves("u2", 20992, [128, 4, 128])
        v1 = halves("v1", 22016, [64, 512])
        v2 = halves("v2", 23040, [128, 512])
        z1 = halves("z1", 24064, [64, 512])
        z2 = halves("z2", 25088, [128, 512])
        wq = place("wq", 26112, [128, 4, 512])
        qTd = halves("qT", 1024, [128, RQ, 2, 512])
        qr = place("qr", 0, [128, 2, 512])
        wor = place("wor", 7168, [128, 2, 512])
        ksd = halves("ks", 8192, [128, 2, 2, 320])
        Sp = place("Sp", 10752, [128, RS, 320])
        Pp = place("Pp", 11712, [128, RP, 384])
        PT = place("PT", 13248, [128, RT, 384])
        Os = place("Os", 14400, [128, 2, 256])
        oTd = halves("oT", 14912, [128, 2, 2, 2, 128])
        Fo = place("Fo", 16960, [128, 2, 512])
        mask = place("mask", 17984, [128, 2, 320])
        KVn = place("KVn", 18624, [128, 4, 512])
        wo = halves("wo", 20672, [128, 4, 512])

        def slot(i):
            return KVo[:, i, :, :]

        xs = x3T[:, :, 1536:2048]
        wt = x3T[:, :, 1024:1536]
        wp = slot(0)
        wkr = slot(0)
        d1r = slot(1)
        d2r = slot(2)
        last = slot(3).rearrange("p a n -> p (a n)")
        w0 = last[:, 0:1024].rearrange("p (a b n) -> p a b n", a=2, b=4)
        u2r = last[:, 1024:1536].rearrange("p (k n) -> p k n", k=4)
        v2r = last[:, 1536:2048]

        def stage(G):
            return x3T[:, G // 2, 512 + (G % 2) * 256:768 + (G % 2) * 256].rearrange("p (a n) -> p a n", n=64)

        tmp = slot(1).rearrange("p a n -> p (a n)")
        tmq = slot(2).rearrange("p a n -> p (a n)")
        E = tmp[0:32, 0:672].rearrange("p (i b) -> p i b", b=32)
        r336 = tmp[0:32, 672:1008]
        w336 = tmp[0:32, 1008:1344]
        CA = tmp[:, 1344:1504]
        CB = tmp[0:32, 1504:1664]
        MA = tmq[:, 0:672]
        MB = tmq[0:32, 672:1344]
        idx = x3T[:, 3, 512:1024]
        rows = tmp[0:32, 1664:1920]
        win = tmq[0:32, 1344:1664]
        wine = tmq[0:32, 1664:1984]
        small = sb("small", [128, 160])
        ti = sb("ti", [128, 24], I32)
        blk = sb("blk", [32, 21], I32)
        kvf = small[:, 0:1]
        rf = small[:, 1:2]
        oh = small[0:32, 2:18]
        blkf = small[0:32, 18:39]
        bwA = small[:, 39:40]
        bwB = small[0:32, 40:41]
        tA = small[:, 41:57]
        vA = small[:, 57:73]
        gA = small[:, 73:89]
        tB = small[0:32, 89:105]
        vB = small[0:32, 105:121]
        gB = small[0:32, 121:137]
        VA = small[:, 137:153]
        ones = sb("ones", [32, 128])
        VB = sb("VB", [32, 16])

        ringA = Ring(psum)
        ringS = Ring(psum[0:2])
        ringT = Ring(psum[2:6])
        ringO = Ring([psum[6]])
        ringF = Ring([psum[7]])

        block = ctx.enter_context(nc.Block())

        PAIRS = range(NPAIR)
        HEADS = [(b, g) for b in range(NB) for g in range(4)]

        @block.tensor
        def _(pe):
            def need(*key):
                book.need(pe, "pe", *key)

            def done(ins, *key):
                book.done(ins, "pe", *key)

            mm, tr = nc.tensor.matmul, nc.tensor.transpose

            def three(ps, w, x, start, stop):
                mm(ps, w[1], x[0], start=start, stop=False)
                mm(ps, w[0], x[1], start=False, stop=False)
                return mm(ps, w[0], x[0], start=False, stop=stop)

            def part(t, *ix):
                return tuple(a[ix] for a in t)

            ALL = slice(None)

            def layer0(G):
                need("ld", "x", G)
                need("w0", G)
                for fc in range(4):
                    ps = ringA.take(need, ("x1", G, fc), [("x1c", G, fc)])
                    for p in range(4):
                        ins = mm(ps[:, p * 128:(p + 1) * 128], xs[:, p, fc * 128:(fc + 1) * 128], w0[:, G % 2, p, :],
                                 start=True, stop=True)
                    done(ins, "x1", G, fc)

            def factors():
                need("ld", "wt")
                need("ld", "at")
                ps = ringA.take(need, ("u1",), [("u1c",)])
                for i in range(4):
                    for j in range(4):
                        ins = mm(ps[:, i * 64:(i + 1) * 64], wt[:, j, i * 128:(i + 1) * 128], at[:, j, :],
                                 start=(j == 0), stop=(j == 3))
                done(ins, "u1")
                need("ld", "wp")
                need("ld", "bt")
                ps = ringA.take(need, ("v1",), [("v1c",)])
                for j in range(4):
                    ins = mm(ps[0:64, :], bt[:, j, :], wp[:, j, :], start=(j == 0), stop=(j == 3))
                done(ins, "v1")

            def low(G, s, src, dense, u, z, v, M):
                pre = ("x1c", "x2c")[s - 1]
                R = slice(0, M)
                ps = ringA.take(need, (f"z{s}", G), [(f"z{s}c", G)])
                need(f"u{s}c")
                for k in range(4):
                    need(pre, G, k)
                    ins = three(ps[0:M, :], part(u, ALL, k, ALL), part(src, ALL, k, ALL), k == 0, k == 3)
                done(ins, f"z{s}", G)
                need(f"d{s}")
                for o in range(4):
                    C = slice(o * 128, o * 128 + 128)
                    ps = ringA.take(need, (f"x{s + 1}", G, o), [(f"x{s + 1}c", G, o), (f"x{s + 1}f", G, o)][:s])
                    for k in range(4):
                        three(ps[:, :], part(dense, ALL, k, C), part(src, ALL, k, ALL), k == 0, False)
                    need(f"v{s}c")
                    need(f"z{s}c", G)
                    ins = three(ps[:, :], part(v, R, C), part(z, R, ALL), False, True)
                    done(ins, f"x{s + 1}", G, o)

            def kv(p):
                G = p // 4
                C = slice((p % 4) * 128, (p % 4) * 128 + 128)
                ps = ringA.take(need, ("kv", p), [("kvv", p), ("ksq", p), ("ky", p)])
                for k in range(4):
                    need("x3c", G, k)
                    ins = three(ps[:, :], part(x13, ALL, k, C), part(wkv, ALL, k, ALL), k == 0, k == 3)
                done(ins, "kv", p)

            def q(p, chunks=(0, 1, 2, 3)):
                if 0 in chunks:
                    (ringA if p < 3 else ringF).take(need, ("q", p), [("qsq", p), ("qy" if p < 3 else "qcopy", p)])
                ps = (ringA if p < 3 else ringF).where[("q", p)]
                for k in chunks:
                    need("x3f", p // 4, k)
                    ins = mm(ps[:, :], x3T[:, k, p * 128:(p + 1) * 128], wq[:, k, :], start=(k == 0), stop=(k == 3))
                if 3 in chunks:
                    done(ins, "q", p)

            def qt(p):
                need("qr", p)
                ps = ringT.take(need, ("qt", p), [("qtc", p)])
                for gp in range(2):
                    for h in range(2):
                        o = ps[:, gp * 256:(gp + 1) * 256].rearrange("p (b h t) -> p h b t", b=2, h=2)[:, h]
                        ins = tr(o, qr[:, p % 2, h * 256 + gp * 128:h * 256 + gp * 128 + 128], ident)
                done(ins, "qt", p)

            def index_old():
                need("rows")
                ps = ringA.take(need, ("io",), [("ioc",)])
                for j in range(2):
                    ins = tr(ps[:, j * 32:(j + 1) * 32], rows[:, j * 128:(j + 1) * 128], c("ident", 0, 32)[:, 0:32])
                done(ins, "io")

            def index_spread():
                need("E")
                ps0 = ringA.take(need, ("spA",), [("MA0",), ("MB0",)])
                mm(ps0[:, 0:320], ones[:, :], E[:, 0:10, :], start=True, stop=True)
                ps1 = ringA.take(need, ("spB",), [("MA1",), ("MB1",), ("CA",), ("CB",)])
                mm(ps1[:, 0:352], ones[:, :], E[:, 10:21, :], start=True, stop=True)
                ps = ringA.take(need, ("bw",), [("bwc",), ("bwd",)])
                mm(ps[:, 0:1], E[:, 16:20, :], ones[:, 0:1], start=True, stop=True)
                ins = mm(ps[0:32, 8:9], E[:, 20, :], ones[:, 0:1], start=True, stop=True)
                done(ins, "bw")

            def index_kill():
                need("CA")
                need("CB")
                need("vA")
                need("vB")
                ps = ringA.take(need, ("kill",), [("VA",), ("VB",)])
                mm(ps[:, 0:16], CA[:, 0:128], vA, start=True, stop=False)
                mm(ps[:, 0:16], CB[:, 0:128], vB, start=False, stop=True)
                mm(ps[0:32, 16:32], CA[:, 128:160], vA, start=True, stop=False)
                ins = mm(ps[0:32, 16:32], CB[:, 128:160], vB, start=False, stop=True)
                done(ins, "kill")

            def index_win():
                for k in ("VA", "VB", "MA0", "MB0", "MA1", "MB1"):
                    need(k)
                ps = ringA.take(need, ("win",), [("w336",)])
                for i in range(21):
                    mm(ps[0:32, i * 16:(i + 1) * 16], MA[:, i * 32:(i + 1) * 32], VA, start=True, stop=False)
                    ins = mm(ps[0:32, i * 16:(i + 1) * 16], MB[:, i * 32:(i + 1) * 32], VB[:, :], start=False, stop=True)
                done(ins, "win")

            def index_winT():
                need("wine")
                i32 = c("ident", 0, 32)[:, 0:32]
                ps = ringA.take(need, ("winT",), [("iwc",), ("inwc",), ("inwd",)])
                for j in range(2):
                    tr(ps[:, j * 32:(j + 1) * 32], wine[:, j * 128:(j + 1) * 128], i32)
                ins = tr(ps[0:64, 64:96], wine[:, 256:320], i32)
                done(ins, "winT")

            need("ld", "cf")
            layer0(0)
            factors()
            for G in range(NG):
                low(G, 1, x13, d1, u1, z1, v1, 64)
                if G == 2:
                    index_win()
                if G == 3:
                    index_winT()
                    need("ld", "wq")
                    q(0)
                    q(1)
                low(G, 2, x2T, d2, u2, z2, v2, 128)
                if G == 0:
                    need("wkv")
                if G == 1:
                    index_old()
                    index_spread()
                for p in range(4 * G, 4 * G + 4):
                    kv(p)
                    if p == 5:
                        index_kill()
                if G < NG - 1:
                    layer0(G + 1)

            def keys(b):
                p, h = b // 2, b % 2
                for c_ in range(2):
                    need("old", b, c_)
                    need("patch", b, c_)
                need("new", p)
                for gp in range(2):
                    ps = ringT.take(need, ("kt", b, gp), [("ktc", b, gp)])
                    for c_ in range(2):
                        tr(ps[:, c_ * 128:(c_ + 1) * 128], KVo[:, p % RO, h * 2 + c_, gp * 128:(gp + 1) * 128], ident)
                    hs = slice(h * 64, h * 64 + 64)
                    ins = tr(ps[:, 256:320], KVn[hs, p % 4, gp * 128:(gp + 1) * 128], c("ident", h * 64, h * 64 + 64)[:, hs])
                    done(ins, "kt", b, gp)

            def scores(n):
                b, g = HEADS[n]
                p, h, gp, g2 = b // 2, b % 2, g // 2, g % 2
                need("qtc", p)
                need("ktc", b, gp)
                ps = ringS.take(need, ("s", n), [("sp", n)])
                C = slice(gp * 256 + h * 128, gp * 256 + h * 128 + 128)
                ins = three(ps[:, 0:320], part(qTd, ALL, p % RQ, g2, C), part(ksd, ALL, b % 2, gp, ALL), True, True)
                done(ins, "s", n)

            def turn(n):
                b, g = HEADS[n]
                need("exp", n)
                ps = ringT.take(need, ("pt", n), [("ptc", n)])
                for c_ in range(2):
                    tr(ps[:, c_ * 128:(c_ + 1) * 128], Pp[:, n % RP, c_ * 128:(c_ + 1) * 128], ident)
                a = 256 - 64 * (b % 2)
                ins = tr(ps[:, 256:384], Pp[:, n % RP, a:a + 128], ident)
                done(ins, "pt", n)

            def values(n):
                b, g = HEADS[n]
                p, h = b // 2, b % 2
                if g == 0:
                    ringO.take(need, ("o", b), [("oc", b)])
                ps = ringO.where[("o", b)]
                need("ptc", n)
                o = ps[:, g * 64:(g + 1) * 64]
                for c_ in range(2):
                    mm(o, PT[:, n % RT, c_ * 128:(c_ + 1) * 128], KVo[:, p % RO, h * 2 + c_, 256 + g * 64:320 + g * 64],
                       start=(c_ == 0), stop=False)
                hs = slice(h * 64, h * 64 + 64)
                ins = mm(o, PT[hs, n % RT, 256:384], KVn[hs, p % 4, 256 + g * 64:320 + g * 64], start=False, stop=True)
                done(ins, "pv", n)

            def turn_out(b):
                need("oc", b)
                ps = ringT.take(need, ("ot", b), [("otc", b)])
                for gp in range(2):
                    ins = tr(ps[:, gp * 128:(gp + 1) * 128], Os[:, b % 2, gp * 128:(gp + 1) * 128], ident)
                done(ins, "ot", b)

            def final(p, k):
                if k == 0:
                    need("wo", 0)
                    need("wo", 1)
                    ps = ringF.take(need, ("f", p), [("fc", p)])
                    for j in range(4):
                        mm(ps[:, j * 128:(j + 1) * 128], x3T[:, j, p * 128:(p + 1) * 128], ident, is_transpose=True,
                           start=(j == 0), stop=False, skip_group_check=True)
                    need("otc", 2 * p)
                    need("otc", 2 * p + 1)
                ps = ringF.where[("f", p)]
                w = part(oTd, ALL, p % 2, k // 2, k % 2, ALL)
                x = part(wo, ALL, k, ALL)
                for i, j in ((1, 0), (0, 1), (0, 0)):
                    ins = mm(ps[:, :], w[i], x[j], start=False, stop=(k == 3 and i == j), skip_group_check=True)
                if k == 3:
                    done(ins, "f", p)

            q(2)
            for ring in (ringS, ringT, ringO, ringF):
                ring.readers = [ringA.readers[psum.index(bank)] for bank in ring.banks]
            qt(0)
            qt(1)
            q(3)
            keys(0)
            for n in range(NSTEP):
                if n < 128:
                    scores(n)
                if 0 <= n - LT < 128:
                    turn(n - LT)
                if 0 <= n - LV < 128:
                    values(n - LV)
                if n % 8 == 5 and 2 <= n // 8 + 1 < NPAIR:
                    qt(n // 8 + 1)
                if n % 4 == 1 and n // 4 + 1 < NB:
                    keys(n // 4 + 1)
                if n >= LO and (n - LO) % 4 == 0 and (n - LO) // 4 < NB:
                    turn_out((n - LO) // 4)
                if n % 8 in (3, 4, 5) and 4 <= n // 8 + 2 < NPAIR:
                    q(n // 8 + 2, ((0,), (1,), (2, 3))[n % 8 - 3])
                p, k = divmod(n - LF, 8)
                if 0 <= p < NPAIR and k < 4:
                    final(p, k)

        @block.scalar
        def _(act):
            def need(*key):
                book.need(act, "act", *key)

            def done(ins, *key):
                book.done(ins, "act", *key)

            def high(dst, src, *key):
                ins = nc.scalar.copy(dst, src)
                done(ins, *key)

            def x1c(G):
                if G >= 1:
                    need("kv", 4 * G - 1)
                for fc in range(4):
                    need("x1", G, fc)
                    high(x13[0][:, fc, :], ringA.where[("x1", G, fc)][:, :], "x1h", G, fc)

            def qsquare(p):
                need("q", p)
                need("kss", 15 if p >= 2 else 11)
                if p >= 1:
                    need("qss", p - 1)
                done(nc.scalar.square(sq[:, :], (ringA if p < 3 else ringF).where[("q", p)][:, :]), "qsq", p)
                if p >= 3:
                    need("qsum", p - 1)
                    done(nc.scalar.copy(yy[:, :], ringF.where[("q", p)][:, :]), "qcopy", p)

            def qroot(p):
                qsquare(p)
                need("qs1", p)
                done(nc.scalar.sqrt(ss[:, 1, :], ss[:, 1, :]), "qroot", p)

            x1c(0)
            need("u1")
            high(u1[0][:, :, :].rearrange("p a b -> p (a b)"), ringA.where[("u1",)][:, 0:256], "u1h")
            need("d1i")
            for k in range(4):
                high(d1[0][:, k, :], d1r[:, k, :], "d1h", k)
            def new_v(p):
                need("ky", p)
                if p >= 2:
                    need("ld", "n", p - 2)
                done(nc.scalar.copy(nt[:, p % 2, 256:512], ringA.where[("kv", p)][:, 256:512]), "kvv", p)

            for G in range(NG):
                for o in range(4):
                    need("x2", G, o)
                    high(x2T[0][:, o, :], ringA.where[("x2", G, o)][:, :], "x2h", G, o)
                    if G == 0 and o == 0:
                        need("d2i")
                        for k in range(4):
                            high(d2[0][:, k, :], d2r[:, k, :], "d2h", k)
                for o in range(4):
                    if G == 3 and o < 2:
                        qroot(o)
                    need("x3", G, o)
                    high(x13[0][:, o, :], ringA.where[("x3", G, o)][:, :], "x3h", G, o)
                    done(nc.scalar.copy(x3T[:, o, G * 512:(G + 1) * 512], ringA.where[("x3", G, o)][:, :]), "x3f", G, o)
                    if G == 0 and o == 0:
                        need("ld", "wkv")
                        for k in range(4):
                            high(wkv[0][:, k, :], wkr[:, k, :], "wkvh", k)
                if G == 0:
                    need("ang")
                    for n in range(2):
                        ins = nc.scalar.activation(sc[:, n, :], (sq, yy)[n][:, :], ACT.Sin)
                    done(ins, "sincos")
                    need("sincos")
                for p in range(4 * G, 4 * G + 4):
                    if p % 4 == LATE and G + 1 < NG:
                        new_v(p - 1)
                        x1c(G + 1)
                    need("kv", p)
                    if p >= 1:
                        need("kss", p - 1)
                    if p == 12:
                        need("qss", 1)
                    done(nc.scalar.square(sq[:, 0:256], ringA.where[("kv", p)][:, 0:256]), "ksq", p)
                    need("ks1", p)
                    kr = ss[:, 2 * (p % 2), 0:4]
                    done(nc.scalar.sqrt(kr, kr), "kroot", p)
                    if p % 4 > 0 and not (p % 4 == LATE and G + 1 < NG):
                        new_v(p - 1)
                    if p % 4 == 3:
                        new_v(p)

            def qtc(p):
                need("qt", p)
                need("qzero")
                if p >= RQ:
                    need("s", 8 * (p - RQ) + 7)
                for g2 in range(2):
                    a = slice(g2 * 64, g2 * 64 + 64)
                    ins = nc.scalar.copy(qTd[0][a, p % RQ, g2, :], ringT.where[("qt", p)][a, :])
                done(ins, "qth", p)

            def split_wo(i):
                need("ld", "wo", i)
                for k in range(2):
                    ins = nc.scalar.copy(wo[0][:, 2 * i + k, :], wor[:, k, :])
                done(ins, "woh", i)

            def kth(b, gp):
                need("kt", b, gp)
                if b >= 2:
                    need("s", 4 * (b - 2) + 1 + 2 * gp)
                done(nc.scalar.copy(ksd[0][:, b % 2, gp, :], ringT.where[("kt", b, gp)][:, 0:320]), "kth", b, gp)

            need("kv", 15)
            qroot(2)
            qtc(0)
            qtc(1)
            split_wo(0)
            qsquare(3)
            kth(0, 0)
            kth(0, 1)
            for n in range(NSTEP + 1):
                p, k = divmod(n - LF, 8)
                if 0 <= p < NPAIR and k == 4:
                    need("f", p)
                    if p >= 2:
                        need("ld", "out", p - 2)
                    done(nc.scalar.copy(Fo[:, p % 2, :], ringF.where[("f", p)][:, :]), "fc", p)
                m = n - 1
                if 0 <= m < 128:
                    need("sp", m)
                    need("pzero")
                    if m >= RP:
                        need("pt", m - RP)
                    done(nc.scalar.activation(Pp[:, m % RP, 0:320], Sp[:, m % RS, :], ACT.Exp, bias=nmx[:, m:m + 1],
                                              scale=-1.0, accum_out=sm[:, m:m + 1]), "exp", m)
                m = n - LT
                if 0 <= m < 128 and m % 2 == 0:
                    need("pt", m)
                    if m >= RT:
                        need("pv", m - RT)
                    done(nc.scalar.copy(PT[:, m % RT, :], ringT.where[("pt", m)][:, 0:384]), "ptc", m)
                if n % 8 == 6 and 4 <= n // 8 + 2 < NPAIR:
                    qsquare(n // 8 + 2)
                if n % 8 == 5 and 2 <= n // 8 + 1 < NPAIR:
                    qtc(n // 8 + 1)
                if n % 4 == 1 and n // 4 + 1 < NB:
                    kth(n // 4 + 1, 0)
                    kth(n // 4 + 1, 1)
                if n == 4:
                    split_wo(1)
                if n >= LO and (n - LO) % 4 == 0 and (n - LO) // 4 < NB:
                    b = (n - LO) // 4
                    need("ot", b)
                    if b >= 4:
                        need("f", b // 2 - 2)
                    for gp in range(2):
                        ins = nc.scalar.copy(oTd[0][:, (b // 2) % 2, gp, :, (b % 2) * 64:(b % 2) * 64 + 64],
                                             ringT.where[("ot", b)][:, gp * 128:(gp + 1) * 128].rearrange(
                                                 "p (h t) -> p h t", h=2))
                    done(ins, "oth", b)

        @block.vector
        def _(dve):
            def need(*key):
                book.need(dve, "dve", *key)

            def done(ins, *key):
                book.done(ins, "dve", *key)
                return key

            v = nc.vector
            ALL = slice(None)

            def step(ins, *key):
                done(ins, *key)
                need(*key)

            def lag(ins, *key):
                done(ins, *key)
                yield
                need(*key)

            def go(chain, n):
                for _ in range(n):
                    next(chain, None)

            need("ld", "ci")
            done(v.tensor_scalar(w0i[:, :], cint("cond"), 64, None, ALU.mult), "w0i0")
            step(v.tensor_scalar(ti[:, 0:1], cint("kvw"), 4, None, ALU.arith_shift_right), "ti0")
            done(v.tensor_scalar(ti[:, 1:2], cint("kvw"), 15, None, ALU.bitwise_and), "ti1")
            done(v.tensor_tensor(w0i[:, :], w0i[:, :], cint("c").to_broadcast([128, 16]), ALU.add), "w0i")
            done(v.tensor_tensor(ti[:, 2:3], ti[:, 0:1], cint("b257"), ALU.add), "ti")
            done(v.memset(w0[:, :, :, :], 0.0), "w0z")
            done(v.memset(ones[:, :], 1.0), "ones")
            need("ti1")
            need("ld", "cf")
            need("ld", "fs")
            step(v.tensor_copy(rf, ti[:, 1:2]), "rf")
            step(v.tensor_scalar(oh, c("iota16", 0, 32), rf[0:32, :], None, ALU.is_equal), "oh")
            done(v.tensor_scalar(mk1[:, :], cint("idx1", 0, 64), c("e", 0, 64), None, ALU.is_equal), "mk1")
            done(v.tensor_scalar(mk2[:, :], cint("idx2"), c("e"), None, ALU.is_equal), "mk2")
            done(v.tensor_scalar(thr[:, :], cint("kvall"), -256.0, BIGC, ALU.add, ALU.mult), "thr")
            need("w0z")

            def blockdiag(G):
                need("ld", "stage", G)
                if G >= 2:
                    need("x1", G - 2, 3)
                for h in range(2):
                    a = slice(h * 64, h * 64 + 64)
                    idb = c("ident", h * 64, h * 64 + 64)[:, a]
                    ins = v.tensor_tensor(w0[a, G % 2, :, a], stage(G)[a, :, :],
                                          idb.unsqueeze(1).to_broadcast([64, 4, 64]), ALU.add)
                done(ins, "w0", G)

            blockdiag(0)
            def low_half(t, ix, src, *key):
                done(v.tensor_tensor(t[1][ix], src, t[0][ix], ALU.subtract), *key)

            def x1l(G):
                for fc in range(4):
                    need("x1h", G, fc)
                    low_half(x13, (ALL, fc, ALL), ringA.where[("x1", G, fc)][:, :], "x1c", G, fc)

            def with_identity(nm, raw):
                need("ld", nm)
                for k in range(4):
                    o = raw[:, k, k * 128:(k + 1) * 128]
                    ins = v.tensor_tensor(o, o, ident, ALU.add)
                done(ins, nm + "i")

            def lows(nm, t, raw):
                for k in range(4):
                    need(nm + "h", k)
                    ins = v.tensor_tensor(t[1][:, k, :], raw[:, k, :], t[0][:, k, :], ALU.subtract)
                done(ins, nm)

            x1l(0)
            for n, nm in enumerate(("qs", "ks")):
                s2 = f(nm).rearrange("p (a b) -> p a b", a=2)
                v.tensor_scalar(gg[:, 2 * n, :, :], s2, 1.0, 8.0, ALU.add, ALU.mult)
                v.tensor_scalar(gg[:, 2 * n + 1, 0, :], s2[:, 1, :], 1.0, -8.0, ALU.add, ALU.mult)
                ins = v.tensor_scalar(gg[:, 2 * n + 1, 1, :], s2[:, 0, :], 1.0, 8.0, ALU.add, ALU.mult)
            done(ins, "gg")
            with_identity("d1", d1r)
            need("u1h")
            u = [t[:, :, :].rearrange("p a b -> p (a b)") for t in u1]
            done(v.tensor_tensor(u[1], ringA.where[("u1",)][:, 0:256], u[0], ALU.subtract), "u1c")
            lows("d1", d1, d1r)
            need("v1")
            step(v.tensor_scalar(t1[0:64, :], ringA.where[("v1",)][0:64, :], f("s1", 0, 64), None, ALU.mult), "v1s")
            step(v.tensor_copy(v1[0][:, :], t1[0:64, :]), "v1h")
            done(v.tensor_tensor(v1[1][:, :], t1[0:64, :], v1[0][:, :], ALU.subtract), "v1c")
            def cache_rows():
                need("ld", "blk")
                yield from lag(v.tensor_copy(blkf, blk[:, :]), "blkf")
                yield from lag(v.scalar_tensor_tensor(r336.rearrange("p (i o) -> p i o", o=16),
                                            blkf.unsqueeze(2).to_broadcast([32, 21, 16]), 16.0,
                                            c("iota16", 0, 32).unsqueeze(1).to_broadcast([32, 21, 16]), ALU.mult, ALU.add), "r336")
                done(v.tensor_tensor(E, blkf.unsqueeze(2).to_broadcast([32, 21, 32]),
                                     c("ident", 0, 32)[:, 0:32].unsqueeze(1).to_broadcast([32, 21, 32]), ALU.mult), "E")
                yield from lag(v.tensor_scalar(rows, r336[:, 0:256], oh[:, 0:1], None, ALU.mult), "rows", 0)
                for k in range(1, 16):
                    yield from lag(v.scalar_tensor_tensor(rows, r336[:, k:k + 256], oh[:, k:k + 1], rows, ALU.mult, ALU.add), "rows", k)
                done(v.tensor_copy(kvf, rf), "rows")

            def writers():
                for nm, P, t_, v_, g_, m16, val in (("A", 128, tA, vA, gA, "m16", "val"), ("B", 32, tB, vB, gB, "m16b", "valb")):
                    yield from lag(v.tensor_scalar(t_, c("iota16", 0, P), c(m16, 0, P), rf[0:P, :], ALU.add, ALU.subtract), "t", nm)
                    v.tensor_scalar(v_, t_, 0.0, None, ALU.is_ge)
                    yield from lag(v.tensor_scalar(g_, t_, 63.0, None, ALU.is_le), "le", nm)
                    yield from lag(v.tensor_tensor(v_, v_, g_, ALU.mult), "v" + nm)
                    yield from lag(v.tensor_scalar(g_, t_, c(val, 0, P), None, ALU.add), "g", nm)

            def match():
                need("bw")
                v.tensor_copy(bwA, ringA.where[("bw",)][:, 0:1])
                done(v.tensor_copy(bwB, ringA.where[("bw",)][0:32, 8:9]), "bwc")
                need("bwc")
                book.new[("bwd",)] = book.new[("bwc",)]
                a, b_ = ringA.where[("spA",)], ringA.where[("spB",)]
                done(v.tensor_scalar(MA[:, 0:320], a[:, 0:320], bwA, None, ALU.is_equal), "MA0")
                done(v.tensor_scalar(MA[:, 320:672], b_[:, 0:352], bwA, None, ALU.is_equal), "MA1")
                done(v.tensor_scalar(MB[:, 0:320], a[0:32, 0:320], bwB, None, ALU.is_equal), "MB0")
                done(v.tensor_scalar(MB[:, 320:672], b_[0:32, 0:352], bwB, None, ALU.is_equal), "MB1")
                done(v.scalar_tensor_tensor(CA, b_[:, 192:352], bwA, c("la"), ALU.is_equal, ALU.mult), "CA")
                done(v.scalar_tensor_tensor(CB, b_[0:32, 192:352], bwB, c("lb", 0, 32), ALU.is_equal, ALU.mult), "CB")

            def survive():
                need("kill")
                ps = ringA.where[("kill",)]
                for nm, P, o, t_, v_, g_, V in (("A", 128, 0, tA, vA, gA, VA), ("B", 32, 16, tB, vB, gB, VB[:, :])):
                    step(v.tensor_scalar(t_, ps[0:P, o:o + 16], 0.0, None, ALU.is_equal), "alive", nm)
                    step(v.tensor_tensor(t_, t_, v_, ALU.mult), "alive2", nm)
                    done(v.tensor_tensor(V, t_, g_, ALU.mult), "V" + nm)

            def winners():
                yield from lag(v.tensor_scalar(win, w336[:, 0:320], oh[:, 0:1], None, ALU.mult), "winner", 0)
                for k in range(1, 16):
                    w = min(320, 336 - k)
                    yield from lag(v.scalar_tensor_tensor(win[:, 0:w], w336[:, k:k + w], oh[:, k:k + 1], win[:, 0:w], ALU.mult,
                                                ALU.add), "winner", k)
                yield from lag(v.tensor_scalar(wine, win, 0.0, SKIP, ALU.is_equal, ALU.mult), "wine0")
                yield from lag(v.scalar_tensor_tensor(wine, win, -1.0, wine, ALU.add, ALU.add), "wine")

            def indices():
                need("winT")
                ps = ringA.where[("winT",)]
                done(v.tensor_copy(iw[:, :, :].rearrange("p a b -> p (a b)"), ps[:, 0:64]), "iwc")
                pr = ps[0:64, 64:96].rearrange("p (a b) -> p b a", b=2)
                done(v.tensor_copy(inw[0:64, :], pr[:, 0, :]), "inwc")
                done(v.tensor_copy(inw[64:128, :], pr[:, 1, :]), "inwd")

            def zc(G, s, z, mk, M):
                need(f"z{s}", G)
                need("v1c")
                need("mk1")
                need("mk2")
                step(v.tensor_tensor(t1[0:M, :].rearrange("p (b t) -> p b t", b=8),
                                     ringA.where[(f"z{s}", G)][0:M, :].rearrange("p (b t) -> p b t", b=8),
                                     mk[0:M, 8 * G:8 * G + 8].unsqueeze(2).to_broadcast([M, 8, 64]), ALU.mult), f"z{s}m", G)
                step(v.tensor_copy(z[0][0:M, :], t1[0:M, :]), f"z{s}h", G)
                done(v.tensor_tensor(z[1][0:M, :], t1[0:M, :], z[0][0:M, :], ALU.subtract), f"z{s}c", G)

            def rope(kind, p, nh, dst, parts=(0, 1, 2, 3)):
                w = nh * 64
                k0 = kind[0]
                r = ss[:, 2 * (p % 2) if k0 == "k" else 1, 0:nh]
                y = yy[:, 0:w].rearrange("p (h a d) -> p h a d", a=2, d=32)
                a, b_ = tr_[:, 0, :, :], tr_[:, 1, :, :]
                if 0 in parts:
                    need(k0 + "sq", p)
                    step(v.tensor_reduce(r, sq[:, 0:w].rearrange("p (h d) -> p h d", d=64), AX.X, ALU.add), k0 + "ss", p)
                    done(v.tensor_scalar(r, r, 64e-6, None, ALU.add), k0 + "s1", p)
                if 1 in parts:
                    o = 0 if k0 == "q" else 2
                    for i in range(2):
                        v.tensor_tensor(tr_[:, i, :, :], sc[:, 1 - i, 32 * p:32 * p + 32].unsqueeze(1).to_broadcast([128, 2, 32]),
                                        gg[:, o + i, :, :], ALU.mult)
                    if k0 == "k" or p < 3:
                        need(k0 + "root", p)
                        step(v.reciprocal(r, r), k0 + "s2", p)
                    else:
                        need("qroot", p)
                    if k0 == "q" and p >= 3:
                        need("qcopy", p)
                    done(v.tensor_tensor(yy[:, 0:w].rearrange("p (h d) -> p h d", d=64),
                                         (yy if k0 == "q" and p >= 3 else ringA.where[(kind, p)])[:, 0:w].rearrange(
                                             "p (h d) -> p h d", d=64),
                                         r.unsqueeze(2).to_broadcast([128, nh, 64]), ALU.mult), k0 + "y", p)
                if 2 in parts:
                    need(k0 + "y", p)
                    v.tensor_tensor(t1[:, 0:w].rearrange("p (h a d) -> p h a d", a=2, d=32), y,
                                    a.unsqueeze(1).to_broadcast([128, nh, 2, 32]), ALU.mult)
                    t2v = t2[:, 0:w].rearrange("p (h a d) -> p h a d", a=2, d=32)
                    for a_ in range(2):
                        ins = v.tensor_tensor(t2v[:, :, a_, :], y[:, :, 1 - a_, :],
                                              b_[:, a_, :].unsqueeze(1).to_broadcast([128, nh, 32]), ALU.mult)
                    done(ins, k0 + "sum", p)
                if 3 in parts:
                    need(k0 + "sum", p)
                    if k0 == "q" and p >= 2:
                        need("qt", p - 2)
                    done(v.tensor_tensor(dst, t1[:, 0:w], t2[:, 0:w], ALU.add), {"k": "kr", "q": "qr"}[k0], p)

            def rope_q(p, *parts):
                rope("q", p, 8, qr[:, p % 2, :], parts)

            def angles():
                ang = t1[:, :].rearrange("p (a d) -> p a d", a=16)
                kvg = t2[:, 0:16]
                yield from lag(v.tensor_copy(kvg, cint("kvtok")), "kvg0")
                yield from lag(v.tensor_scalar(kvg, kvg, c("t"), None, ALU.add), "kvg")
                yield from lag(v.tensor_tensor(ang, kvg.unsqueeze(2).to_broadcast([128, 16, 32]),
                                     c("inv").unsqueeze(1).to_broadcast([128, 16, 32]), ALU.mult), "ang0")
                A = t1[:, :]
                n_, m_ = idx[:, :], t2[:, :]
                for i, (dst, off) in enumerate(((sq[:, :], 0.0), (yy[:, :], 0.25))):
                    yield from lag(v.tensor_scalar(n_, A, float(1.0 / TWO_PI), off, ALU.mult, ALU.add), "rr", i, 0)
                    yield from lag(v.tensor_scalar(m_, n_, MAGIC, None, ALU.add), "rr", i, 1)
                    yield from lag(v.tensor_scalar(n_, m_, -MAGIC, None, ALU.add), "rr", i, 2)
                    yield from lag(v.scalar_tensor_tensor(dst, n_, -C1, A, ALU.mult, ALU.add), "rr", i, 3)
                    yield from lag(v.scalar_tensor_tensor(m_, n_, -C2, dst, ALU.mult, ALU.add), "rr", i, 4)
                    yield from lag(v.scalar_tensor_tensor(dst, n_, -C3, m_, ALU.mult, ALU.add), "rr", i, 5)
                    if off:
                        yield from lag(v.tensor_scalar(dst, dst, float(np.pi / 2), None, ALU.add), "rr", i, 6)
                    yield from lag(v.tensor_scalar(dst, dst, 3.1415925, -3.1415925, ALU.min, ALU.max), "rr", i, 7)
                done(v.tensor_copy(nmx[:, 0:1], dst[:, 0:1]), "ang")
                need("ang")

            need("gg")
            chain = iter(())
            for G in range(NG):
                if G == 0:
                    zc(0, 1, z1, mk1, 64)
                    blockdiag(1)
                    with_identity("d2", d2r)
                    need("ld", "v2")
                    need("ld", "u2")
                    step(v.tensor_scalar(v2r, v2r, f("s2"), None, ALU.mult), "v2s")
                    v.tensor_copy(v2[0][:, :], v2r)
                    step(v.tensor_copy(u2[0][:, :, :], u2r), "uvh")
                    done(v.tensor_tensor(v2[1][:, :], v2r, v2[0][:, :], ALU.subtract), "v2c")
                    done(v.tensor_tensor(u2[1][:, :, :], u2r, u2[0][:, :, :], ALU.subtract), "u2c")
                if G == 1:
                    chain = cache_rows()
                for o in range(4):
                    need("x2h", G, o)
                    low_half(x2T, (ALL, o, ALL), ringA.where[("x2", G, o)][:, :], "x2c", G, o)
                    if G == 0 and o == 0:
                        lows("d2", d2, d2r)
                    if o < 3:
                        go(chain, 5)
                if G == 1:
                    blockdiag(3)
                if G == 3:
                    indices()
                zc(G, 2, z2, mk2, 128)
                go(chain, 99)
                if G == 0:
                    chain = angles()
                if G == 1:
                    chain = writers()
                if G == 2:
                    need("win")
                    step(v.tensor_copy(w336, ringA.where[("win",)][0:32, 0:336]), "w336")
                    chain = winners()
                for o in range(4):
                    go(chain, 5)
                    if G == 3 and o < 2:
                        rope_q(o, 0, 1, 2, 3)
                    need("x3f", G, o)
                    low_half(x13, (ALL, o, ALL), ringA.where[("x3", G, o)][:, :], "x3c", G, o)
                    if G == 0 and o == 0:
                        lows("wkv", wkv, wkr)
                if G < 2:
                    go(chain, 99)
                if G == 1:
                    need("io")
                    done(v.tensor_copy(io[:, :, :].rearrange("p a b -> p (a b)"), ringA.where[("io",)][:, 0:64]), "ioc")
                    match()
                need("sincos")
                def rope_k(p, *parts):
                    if 3 in parts and p >= 2:
                        need("ld", "n", p - 2)
                    rope("kv", p, 4, nt[:, p % 2, 0:256], parts)

                early = G + 1 < NG
                rope_k(4 * G, 0)
                for p in range(4 * G, 4 * G + 4):
                    if p % 4 == LATE and early:
                        if G == 1:
                            survive()
                        x1l(G + 1)
                        zc(G + 1, 1, z1, mk1, 64)
                        if G == 0:
                            blockdiag(2)
                        rope_k(p, 0)
                    rope_k(p, 1)
                    if p % 4 < 3 and not (p % 4 == LATE - 1 and early):
                        rope_k(p + 1, 0)
                    rope_k(p, 2, 3)
                    go(chain, 1)

            def ktl(b, gp):
                need("kth", b, gp)
                low_half(ksd, (ALL, b % 2, gp, ALL), ringT.where[("kt", b, gp)][:, 0:320], "ktc", b, gp)

            def qtl(p):
                need("qth", p)
                for g2 in range(2):
                    a = slice(g2 * 64, g2 * 64 + 64)
                    ins = v.tensor_tensor(qTd[1][a, p % RQ, g2, :], ringT.where[("qt", p)][a, :], qTd[0][a, p % RQ, g2, :],
                                          ALU.subtract)
                done(ins, "qtc", p)

            def lows_wo(i):
                need("woh", i)
                for k in range(2):
                    ins = v.tensor_tensor(wo[1][:, 2 * i + k, :], wor[:, k, :], wo[0][:, 2 * i + k, :], ALU.subtract)
                done(ins, "wo", i)

            def maskb(b):
                done(v.scalar_tensor_tensor(mask[:, b % 2, 0:256], c("iotac"), thr[:, b:b + 1], c("band")[:, 0:256],
                                            ALU.add, ALU.min), "mask", b)

            need("kv", 15)
            maskb(0)
            rope_q(2, 0, 1, 2)
            qtl(0)
            qtl(1)
            rope_q(2, 3)
            lows_wo(0)
            rope_q(3, 0)
            ktl(0, 0)
            ktl(0, 1)
            for n in range(NSTEP):
                if n < 128:
                    b = n // 4
                    need("s", n)
                    need("mask", b)
                    need("mask0")
                    if n >= RS:
                        need("exp", n - RS)
                    done(v.tensor_tensor_reduce(Sp[:, n % RS, :], ringS.where[("s", n)][:, 0:320], mask[:, b % 2, :],
                                                -0.0625, 3.0e38, ALU.add, ALU.min, nmx[:, n:n + 1]), "sp", n)
                m = n - LT
                if 0 <= m < 128 and m % 2 == 1:
                    need("pt", m)
                    if m >= RT:
                        need("pv", m - RT)
                    done(v.tensor_copy(PT[:, m % RT, :], ringT.where[("pt", m)][:, 0:384]), "ptc", m)
                m = n - LV
                if 0 <= m < 128 and m % 4 == 3:
                    b = m // 4
                    need("exp", m)
                    step(v.reciprocal(rs[:, 4 * b:4 * b + 4], sm[:, 4 * b:4 * b + 4]), "rs", b)
                    need("pv", m)
                    if b >= 2:
                        need("ot", b - 2)
                    done(v.tensor_tensor(Os[:, b % 2, :].rearrange("p (g d) -> p g d", g=4),
                                         ringO.where[("o", b)][:, 0:256].rearrange("p (g d) -> p g d", g=4),
                                         rs[:, 4 * b:4 * b + 4].unsqueeze(2).to_broadcast([128, 4, 64]), ALU.mult), "oc", b)
                if n % 8 == 5 and 2 <= n // 8 + 1 < NPAIR:
                    qtl(n // 8 + 1)
                if n % 4 == 1 and n // 4 + 1 < NB:
                    ktl(n // 4 + 1, 0)
                    ktl(n // 4 + 1, 1)
                    maskb(n // 4 + 1)
                if n == 4:
                    lows_wo(1)
                p, k = divmod(n + 9, 8)
                if 3 <= p < NPAIR and k in (0, 3, 4, 5) and (p, k) != (3, 0):
                    rope_q(p, {0: 0, 3: 1, 4: 2, 5: 3}[k])
                if n >= LO and (n - LO) % 4 == 0 and (n - LO) // 4 < NB:
                    b = (n - LO) // 4
                    need("oth", b)
                    for gp in range(2):
                        ix = (ALL, (b // 2) % 2, gp, ALL, slice((b % 2) * 64, (b % 2) * 64 + 64))
                        ins = v.tensor_tensor(oTd[1][ix], ringT.where[("ot", b)][:, gp * 128:(gp + 1) * 128].rearrange(
                            "p (h t) -> p h t", h=2), oTd[0][ix], ALU.subtract)
                    done(ins, "otc", b)

        @block.gpsimd
        def _(pool):
            def need(*key):
                book.need(pool, "pool", *key)

            off = bass.IndirectOffsetOnAxis

            def rsqrt(p):
                need("qs1", p)
                r, y, a = ss[:, 1, :], nw[:, 0, :], nw[:, 1, :]
                g = nc.gpsimd

                def step(ins, *key):
                    book.done(ins, "pool", *key)
                    need(*key)

                step(g.tensor_scalar(y.bitcast(I32), r.bitcast(I32), -0.5, float(0x5F3759DF), ALU.mult, ALU.add), "nw", p)
                for i in range(3):
                    step(g.tensor_tensor(a, y, y, ALU.mult), "nw", p, i, 2)
                    step(g.tensor_tensor(a, a, r, ALU.mult), "nw", p, i, 3)
                    step(g.tensor_scalar(a, a, -0.5, 1.5, ALU.mult, ALU.add), "nw", p, i, 4)
                    if i < 2:
                        step(g.tensor_tensor(y, y, a, ALU.mult), "nw", p, i, 5)
                    else:
                        book.done(g.tensor_tensor(r, y, a, ALU.mult), "pool", "qroot", p)

            need("w0i")
            for G in range(4):
                for p in range(4 * G, 4 * G + 4):
                    ins = nc.gpsimd.indirect_dma_start(stage(G)[:, p % 4, :], None, W0[:, :],
                                                       off(ap=w0i[:, p:p + 1].bitcast(U32), axis=0))
                    book.done(ins, f"g_w{G}", "stage", p)
                book.new[("ld", "stage", G)] = book.new[("stage", 4 * G + 3)]
                if G == 0:
                    need("ti")
                    ins = nc.gpsimd.indirect_dma_start(blk[:, :], None, TBL[:, :],
                                                       off(ap=ti[0:32, 2:3].bitcast(U32), axis=0))
                    book.done(ins, "g_blk", "ld", "blk")

            def zero():
                need("x3", 3, 3)
                for i in range(2):
                    ins = nc.gpsimd.memset(qTd[i][:, :, :, :].bitcast(F32), 0.0)
                book.done(ins, "pool", "qzero")
                need("kv", 15)
                for r in range(RP):
                    ins = nc.gpsimd.memset(Pp[:, r, 320:384], 0.0)
                book.done(ins, "pool", "pzero")
                for r in range(2):
                    ins = nc.gpsimd.tensor_copy(mask[:, r, 256:320], c("band")[:, 256:320])
                book.done(ins, "pool", "mask0")

            def old(p):
                if p >= RO:
                    need("pv", 8 * (p - RO) + 7)
                for h in range(2):
                    for c_ in range(2):
                        b = 2 * p + h
                        ins = nc.gpsimd.indirect_dma_start(KVo[:, p % RO, h * 2 + c_, :], None, KV[:, :],
                                                           off(ap=io[:, c_, b:b + 1], axis=0))
                        book.done(ins, f"g_o{(p % RO)}_{h}{c_}", "old", b, c_)

            need("ioc")
            need("wkv")
            for p in range(RO):
                if p == 1:
                    need("winT")
                    need("x1", 3, 3)
                    need("u2c")
                    need("v2c")
                old(p)
            need("iwc")
            zero()
            need("inwc")
            need("inwd")
            for p in PAIRS:
                need("ld", "n", p)
            for p in PAIRS:
                if p >= RO:
                    old(p)
                ins = nc.gpsimd.indirect_dma_start(KVn[:, p % 4, :], None, SCR[:, :], off(ap=inw[:, p:p + 1], axis=0))
                book.done(ins, f"g_n{p % 4}", "new", p)
                for h in range(2):
                    for c_ in range(2):
                        b = 2 * p + h
                        need("old", b, c_)
                        ins = nc.gpsimd.indirect_dma_start(KVo[:, p % RO, h * 2 + c_, :], None, SCR[:, :],
                                                           off(ap=iw[:, c_, b:b + 1], axis=0),
                                                           bounds_check=2047, oob_is_err=False)
                        book.done(ins, f"g_p{p % 4}_{h}{c_}", "patch", b, c_)
                if p >= RO:
                    rsqrt(p - 1)
            rsqrt(NPAIR - 1)

        @block.sync
        def _(sp):
            def need(*key):
                book.need(sp, "sp", *key)

            def load(dst, src, *key):
                book.done(nc.sync.dma_start(dst, src), "d_" + "_".join(map(str, key)), "ld", *key)

            load(ci[:, :], CID[:, :], "ci")
            load(cf[:, :], CFD[:, :], "cf")
            load(fs[:, :], FSD[:, :], "fs")
            load(xs, X[:, 0, :, :], "x", 0)
            need("ld", "stage", 0)
            load(wt, WT[:, :, :], "wt")
            load(at[:, :, :], AT[:, :, :], "at")
            load(wp, WP[:, :, :], "wp")
            load(bt[:, :, :], BT[:, :, :], "bt")
            load(d1r, WB[:, :, :], "d1")
            load(u2r, A2[:, :, :], "u2")
            load(v2r, V2D[:, :], "v2")
            load(d2r, W2[:, :, :], "d2")
            load(wq[:, :, :], WQKV[:, :, 0:512], "wq")
            need("v1")
            load(wkr, WQKV[:, :, 512:1024], "wkv")
            for G in range(NG):
                if G + 1 < NG:
                    need("x1", G, 3)
                    load(xs, X[:, G + 1, :, :], "x", G + 1)
                if G == 3:
                    need("x3", 3, 3)
                    load(wor[:, :, :], WO[:, 0:2, :], "wo", 0)
                for p in range(4 * G, 4 * G + 4):
                    need("kr", p)
                    need("kvv", p)
                    load(SCR[p * 128:(p + 1) * 128, :], nt[:, p % 2, :], "n", p)
            need("wo", 0)
            load(wor[:, :, :], WO[:, 2:4, :], "wo", 1)
            for p in PAIRS:
                need("fc", p)
                load(out[p * 128:(p + 1) * 128, :], Fo[:, p % 2, :], "out", p)
            for p in PAIRS:
                need("ld", "out", p)


def _constants():
    cf = np.zeros((128, NCF), np.float32)
    ci = np.zeros((128, 2), np.int32)
    p = np.arange(128)

    def put(name, a):
        lo, hi = CF[name]
        cf[:a.shape[0], lo:hi] = a.reshape(a.shape[0], hi - lo)
    put("ident", np.eye(128, dtype=np.float32))
    t, s = (p % 64)[:, None], np.arange(320)[None, :]
    put("band", np.where((s > t) & (s <= t + 256), 0.0, -1e30))
    put("iotac", np.broadcast_to(np.arange(256) * BIGC, (128, 256)))
    m, b = np.divmod(np.arange(160), 32)
    order = b * 5 + m
    later = (order[:, None] > order[None, :]).astype(np.float32)
    put("la", later[:128])
    put("lb", later[128:])
    put("iota16", np.broadcast_to(np.arange(16.0), (128, 16)))
    half = np.float32(10000.0) ** (np.arange(32, dtype=np.float32) / np.float32(32))
    put("inv", np.broadcast_to((np.float32(1.0) / half).astype(np.float32), (128, 32)))
    put("t", (p % 64).astype(np.float32))
    put("e", (p // 16).astype(np.float32))
    put("m16", (p // 32 * 16.0))
    put("val", (p % 32 * 64.0 + 1))
    put("m16b", np.full(128, 64.0))
    put("valb", (p % 32 * 64.0 + 1))
    ci[:, 0] = p % 64
    ci[:, 1] = p * 257
    return cf, ci


def _layout(i):
    a = {k: np.asarray(v) for k, v in i.items()}
    cf, cc = _constants()
    cond, i1, i2, kv = (a[k].astype(np.int32) for k in ("itok_B_1_198", "itok_B_0_3", "itok_B_0_6", "itok_B_37_3939"))
    ci = np.zeros((128, NCI), np.int32)

    def put(name, v):
        lo, hi = CI[name]
        ci[:, lo:hi] = v

    def by_pair(v):
        return np.repeat(v.reshape(16, 2).T, 64, axis=0)
    put("cond", by_pair(cond))
    put("kvtok", by_pair(kv))
    put("idx1", i1[None, :])
    put("idx2", i2[None, :])
    put("kvall", kv[None, :])
    put("kvw", np.tile(kv, 4)[:, None])
    put("c", cc[:, 0:1])
    put("b257", cc[:, 1:2])
    fs = np.zeros((128, NFS), np.float32)
    fs[:, FS["qs"][0]:FS["qs"][1]] = a["L3_cond_q_norm_scale"][None, :]
    fs[:, FS["ks"][0]:FS["ks"][1]] = a["L3_cond_k_norm_scale"][None, :]
    fs[0:64, FS["s1"][0]] = np.repeat(a["L1_cond_scaling"], 16)
    fs[:, FS["s2"][0]] = np.repeat(a["L2_cond_scalings"], 16)

    def rows(w):
        return np.ascontiguousarray(w.reshape(4, 128, -1).transpose(1, 0, 2))
    tbl = a["itok_Bx257_0_4111"].astype(np.int32)
    at = np.clip(np.arange(257)[:, None] - 16 + np.arange(21)[None, :], 0, 256)
    tbl = np.ascontiguousarray(tbl[:, at].reshape(NB * 257, 21))
    Wq = a["L3_cond_Wq"].reshape(4, 2, 64, 512).transpose(1, 0, 2, 3).reshape(512, 512)
    wqkv = np.concatenate([Wq, a["L3_cond_Wk"], a["L3_cond_Wv"]], 0).T
    wo = a["L3_cond_Wo"].T.reshape(2, 2, 2, 64, 512).transpose(0, 2, 1, 3, 4).reshape(512, 512)
    kvr = np.empty((4112, 16, 2, 4, 64), np.float32)
    kvr[:, :, 0] = a["L3_cond_k_blocks"].transpose(0, 2, 1, 3)
    kvr[:, :, 1] = a["L3_cond_v_blocks"].transpose(0, 2, 1, 3)
    return {
        "X": np.ascontiguousarray(a["x"].reshape(4, 4, 128, 512).transpose(2, 0, 1, 3)),
        "W0": np.ascontiguousarray(a["L0_cond_weights"].reshape(12800, 64)),
        "WB": rows(a["L1_cond_W_base"].T),
        "WT": rows(a["L1_cond_Wt"]),
        "AT": rows(a["L1_cond_A"].reshape(64, 512).T),
        "BT": rows(a["L1_cond_B_w"].transpose(1, 0, 2).reshape(512, 64)),
        "WP": rows(a["L1_cond_Wp"].T),
        "W2": rows(a["L2_cond_W"].T),
        "A2": rows(a["L2_cond_A"].reshape(128, 512).T),
        "V2D": np.ascontiguousarray(a["L2_cond_Bm"].transpose(0, 2, 1).reshape(128, 512)),
        "WQKV": rows(wqkv),
        "WO": rows(wo),
        "KV": kvr.reshape(KVROWS, 512),
        "TBL": tbl,
        "CFD": cf,
        "CID": ci,
        "FSD": fs,
    }


def _build(make, arrays):
    known = None
    for _ in range(2):
        nc = make()
        args = {}
        for name, v in arrays.items():
            args[name] = nc.dram_tensor(f"in_{name}", v.shape, mybir.dt.from_np(v.dtype), kind="ExternalInput").ap()
        args["SCR"] = nc.dram_tensor("scratch", (2048, 512), F32, kind="Internal").ap()
        args["out"] = nc.dram_tensor("out_0_dram", (2048, 512), F32, kind="ExternalOutput").ap()
        book = Book(known)
        program(nc, book, **args)
        known = book.new
    return nc


def kernel(**inputs):
    import concourse.bacc as _bacc
    from concourse.bass_utils import run_bass_kernel_spmd as _run

    arrays = _layout(inputs)
    nc = _build(lambda: _bacc.Bacc("TRN2", target_bir_lowering=False, num_devices=1), arrays)
    r = _run(nc, [{f"in_{k}": v for k, v in arrays.items()}], core_ids=[0])
    return r.results[0]["out_0_dram"].reshape(NB, T, D)
```
